# Optimizing a Trainium2 kernel written in Bass

```python
import numpy as np
import jax
import jax.numpy as jnp

def _softmax(x, axis=-1):
    return jax.nn.softmax(x, axis=axis)

def _gelu(x):
    return jax.nn.gelu(x, approximate=True)

def _silu(x):
    return jax.nn.silu(x)

def _sigmoid(x):
    return jax.nn.sigmoid(x)

def _layernorm(x, axis=-1, eps=1e-05):
    m = jnp.mean(x, axis=axis, keepdims=True)
    v = jnp.var(x, axis=axis, keepdims=True)
    return (x - m) / jnp.sqrt(v + eps)

def _scatter_add(tgt, idx, src, axis=0):
    return tgt.at[idx].add(src)

def _segment_sum(src, seg, n):
    return jax.ops.segment_sum(src, seg, n)
kernel_name = 'mk_adaln_ffn_d1_seqx_r4_36aad2'

def setup_inputs(seed: int=0):
    np.random.seed(seed)
    _w = jnp.asarray

    def _rec_inputs():
        import jax
        import jax.numpy as jnp
        _rk = jax.random.key(seed)
        x = -7.109e-05 + 0.9999 * jax.random.normal(jax.random.fold_in(_rk, 1), (32, 64, 512), jnp.float32)
        _lenS = 64 - jax.random.randint(jax.random.fold_in(_rk, 7), (32,), 0, max(1, 64 // 4) + 1, jnp.int32)
        _lenS2 = 64 - jax.random.randint(jax.random.fold_in(_rk, 8), (32,), 0, max(1, 64 // 4) + 1, jnp.int32)
        itok_B_1_198 = jax.random.randint(jax.random.fold_in(_rk, 11), (32,), 1, 199, jnp.int32)
        return (x, itok_B_1_198)
    x, itok_B_1_198 = _rec_inputs()

    def _L0_cond_setup():
        import jax, jax.numpy as jnp
        import numpy as np
        B, C, T = (128, 64, 512)
        S, D = (200, 64)
        key = jax.random.key(seed)
        k1, k2, k3 = jax.random.split(key, 3)
        x = jax.random.normal(k1, (B, C, T), dtype=jnp.float32)
        conditions = jax.random.randint(k2, (B,), 0, S, dtype=jnp.int64)
        weights = jax.random.normal(k3, (S, C, D), dtype=jnp.float32) / jnp.sqrt(jnp.float32(C))
        return {'x': x, 'conditions': conditions, 'weights': weights}
    _L0_cond_all = _L0_cond_setup()
    _L0_cond_in = {k: v for k, v in _L0_cond_all.items() if k in ('weights',)}
    del _L0_cond_all

    def _L0_ffn_setup():
        import jax, jax.numpy as jnp
        import numpy as np
        BLOCK_SIZE = 32
        HIDDEN_SIZE = 512
        MLP_DIM = 4096
        NVFP4_LUT = jnp.array([0.0, 0.5, 1.0, 1.5, 2.0, 3.0, 4.0, 6.0, 0.0, -0.5, -1.0, -1.5, -2.0, -3.0, -4.0, -6.0], dtype=jnp.float32)

        def dequant_nvfp4(W_packed, scales, block=BLOCK_SIZE):
            N = W_packed.shape[0]
            low = W_packed & 15
            high = W_packed >> 4 & 15
            idx = jnp.stack([low, high], axis=-1).reshape(N, -1)
            vals = NVFP4_LUT[idx]
            K = vals.shape[1]
            vals = vals.reshape(N, K // block, block) * scales[:, :, None]
            return vals.reshape(N, K)
        key = jax.random.key(seed)
        ks = jax.random.split(key, 7)
        x = jax.random.normal(ks[0], (4, 32, HIDDEN_SIZE), dtype=jnp.float32)
        gate_W_packed = jax.random.randint(ks[1], (MLP_DIM, HIDDEN_SIZE // 2), 0, 64, dtype=jnp.int32)
        gate_scales = jax.random.uniform(ks[2], (MLP_DIM, HIDDEN_SIZE // BLOCK_SIZE), dtype=jnp.float32) * 0.1 + 0.001
        up_W_packed = jax.random.randint(ks[3], (MLP_DIM, HIDDEN_SIZE // 2), 0, 64, dtype=jnp.int32)
        up_scales = jax.random.uniform(ks[4], (MLP_DIM, HIDDEN_SIZE // BLOCK_SIZE), dtype=jnp.float32) * 0.1 + 0.001
        down_W_packed = jax.random.randint(ks[5], (HIDDEN_SIZE, MLP_DIM // 2), 0, 64, dtype=jnp.int32)
        down_scales = jax.random.uniform(ks[6], (HIDDEN_SIZE, MLP_DIM // BLOCK_SIZE), dtype=jnp.float32) * 0.1 + 0.001
        return {'x': x, 'gate_W_packed': gate_W_packed, 'gate_scales': gate_scales, 'up_W_packed': up_W_packed, 'up_scales': up_scales, 'down_W_packed': down_W_packed, 'down_scales': down_scales}
    _L0_ffn_all = _L0_ffn_setup()
    _L0_ffn_in = {k: v for k, v in _L0_ffn_all.items() if k in ('gate_W_packed', 'gate_scales', 'up_W_packed', 'up_scales', 'down_W_packed', 'down_scales')}
    del _L0_ffn_all
    return {'x': x, 'itok_B_1_198': itok_B_1_198, 'L0_cond_weights': _L0_cond_in['weights'], 'L0_ffn_gate_W_packed': _L0_ffn_in['gate_W_packed'], 'L0_ffn_gate_scales': _L0_ffn_in['gate_scales'], 'L0_ffn_up_W_packed': _L0_ffn_in['up_W_packed'], 'L0_ffn_up_scales': _L0_ffn_in['up_scales'], 'L0_ffn_down_W_packed': _L0_ffn_in['down_W_packed'], 'L0_ffn_down_scales': _L0_ffn_in['down_scales']}

def reference(x, itok_B_1_198, L0_cond_weights, L0_ffn_gate_W_packed, L0_ffn_gate_scales, L0_ffn_up_W_packed, L0_ffn_up_scales, L0_ffn_down_W_packed, L0_ffn_down_scales):
    import jax
    import jax.numpy as jnp

    def _L0_cond_ref(x, conditions, weights):
        import jax, jax.numpy as jnp
        import numpy as np
        B, C, T = (128, 64, 512)
        S, D = (200, 64)
        w = weights[conditions]
        return jnp.einsum('bct,bcd->bdt', x, w)

    def _L0_ffn_ref(x, gate_W_packed, gate_scales, up_W_packed, up_scales, down_W_packed, down_scales):
        import jax, jax.numpy as jnp
        import numpy as np
        BLOCK_SIZE = 32
        HIDDEN_SIZE = 512
        MLP_DIM = 4096
        NVFP4_LUT = jnp.array([0.0, 0.5, 1.0, 1.5, 2.0, 3.0, 4.0, 6.0, 0.0, -0.5, -1.0, -1.5, -2.0, -3.0, -4.0, -6.0], dtype=jnp.float32)

        def dequant_nvfp4(W_packed, scales, block=BLOCK_SIZE):
            N = W_packed.shape[0]
            low = W_packed & 15
            high = W_packed >> 4 & 15
            idx = jnp.stack([low, high], axis=-1).reshape(N, -1)
            vals = NVFP4_LUT[idx]
            K = vals.shape[1]
            vals = vals.reshape(N, K // block, block) * scales[:, :, None]
            return vals.reshape(N, K)
        B, S, H = x.shape
        xt = x.reshape(B * S, H)
        Wg = dequant_nvfp4(gate_W_packed, gate_scales)
        Wu = dequant_nvfp4(up_W_packed, up_scales)
        Wd = dequant_nvfp4(down_W_packed, down_scales)
        gate = jnp.einsum('th,nh->tn', xt, Wg)
        up = jnp.einsum('th,nh->tn', xt, Wu)
        gelu = jnp.tanh(0.7978845608028654 * (gate + 0.044715 * gate ** 3)) * gate * 0.5 + gate * 0.5
        inter = gelu * up
        out = jnp.einsum('tn,hn->th', inter, Wd)
        return out.reshape(B, S, H)
    x = x + _L0_ffn_ref(_L0_cond_ref(x, itok_B_1_198, L0_cond_weights), L0_ffn_gate_W_packed, L0_ffn_gate_scales, L0_ffn_up_W_packed, L0_ffn_up_scales, L0_ffn_down_W_packed, L0_ffn_down_scales)
    return x

_drawn_inputs = setup_inputs


def setup_inputs(seed=0):
    import zlib

    import numpy as np

    out = dict(_drawn_inputs(seed))
    spreads = {}
    factors = {}
    for name, (base, spread) in spreads.items():
        noise = np.random.default_rng([zlib.crc32(name.encode()), seed]).standard_normal(out[name].shape)
        drawn = base * np.exp(spread * noise) if base else spread * noise
        out[name] = jnp.asarray(drawn.astype(out[name].dtype))
    for name, factor in factors.items():
        out[name] = (out[name] * factor).astype(out[name].dtype)
    return out
```

```python
from contextlib import ExitStack

import concourse.bass as bass
from concourse import mybir

F32 = mybir.dt.float32
F32R = mybir.dt.float32r
F16 = mybir.dt.float16
I32 = mybir.dt.int32
U16 = mybir.dt.uint16
U32 = mybir.dt.uint32
ALU = mybir.AluOpType
ACT = mybir.ActivationFunctionType

P = 128
G = 4
R = 32
N = 512
GELU_C = 0.7978845608028654
GELU_A = 0.044715
CODE_MASK = 0x8E00
CODE_SCALE = float(2 ** 14)


def build(nc, x, itok, cond_w, gate_q, gate_s, up_q, up_s, down_q, down_s, out):
    B, C, H = x.shape
    SAMPLES, _, D = cond_w.shape
    MLP = gate_q.shape[0]
    TOK = B * D
    TG = TOK // N
    TT = TOK // P
    TPG = N // P
    KC = H // P
    SC = MLP // (2 * P)
    BG = 2 * G * KC
    BLK = 3 * BG
    PIECES = 6
    PB = BLK // PIECES
    PW = PB * R
    HP = R // 2
    assert C == 64 and D == 64 and BG == 2 * H // R and TG == 4 and SC % 2 == 0

    ctx = ExitStack()
    with ctx:
        def sb(name, shape, dt):
            return ctx.enter_context(nc.sbuf_tensor(name, shape, dt))

        def sem(name):
            return ctx.enter_context(nc.semaphore(name))

        acc = sb("acc", [P, TT, H], F32)
        h_hi = sb("h_hi", [P, KC, TOK], F32R)
        h_lo = sb("h_lo", [P, KC, TOK], F32R)
        w_hi = sb("w_hi", [P, 2 * BLK, R], F32R)
        w_lo = sb("w_lo", [P, 2 * BLK, R], F32R)
        inter_hi = sb("inter_hi", [P, 2, 2, N], F32R)
        inter_lo = sb("inter_lo", [P, 2, 2, N], F32R)
        packed = sb("packed", [P, 2 * BLK, HP], I32)
        scales = sb("scales", [P, 2 * BLK], F32)
        shifted = sb("shifted", [P, 2, PB * HP], I32)
        codes = sb("codes", [P, 2, PB * HP], U16)
        w_row = sb("w_row", [P, PW], F32)
        w_col = sb("w_col", [P, PW], F32)
        scale_now = sb("scale_now", [P, PB], F32)
        work = sb("work", [P, 3, 2, N], F32)
        poly, tanh, inter = work[:, 0], work[:, 1], work[:, 2]
        mix = sb("mix", [P, TT, D], F32)
        who = sb("who", [P, B], I32)
        held = sb("held", [P, B], I32)
        chan = sb("chan", [P, TT], I32)
        row = sb("row", [P, TT], U32)
        bank = ctx.enter_context(nc.psum_tensor("bank", [P, 8, N], F32))
        gate_ps = [bank[:, 0, :], bank[:, 2, :]]
        up_ps = [bank[:, 1, :], bank[:, 3, :]]

        x_loaded = [sem(f"x_loaded{t}") for t in range(TG)]
        who_loaded = sem("who_loaded")
        chan_made = sem("chan_made")
        who_held = sem("who_held")
        row_made = sem("row_made")
        mix_loaded = [sem(f"mix_loaded{t}") for t in range(TG)]
        packed_loaded = [sem(f"packed_loaded{p}") for p in range(2)]
        x_turned = sem("x_turned")
        h_ready = sem("h_ready")
        h_hi_done = sem("h_hi_done")
        h_lo_done = sem("h_lo_done")
        shift_done = sem("shift_done")
        codes_done = sem("codes_done")
        scale_done = sem("scale_done")
        w_row_done = sem("w_row_done")
        w_col_done = sem("w_col_done")
        w_hi_done = sem("w_hi_done")
        w_lo_done = sem("w_lo_done")
        gate_ready = sem("gate_ready")
        up_ready = sem("up_ready")
        square_done = sem("square_done")
        poly_done = sem("poly_done")
        arg_done = sem("arg_done")
        tanh_done = sem("tanh_done")
        gelu_done = sem("gelu_done")
        inter_done = sem("inter_done")
        inter_hi_done = sem("inter_hi_done")
        inter_lo_done = sem("inter_lo_done")
        down_ready = sem("down_ready")
        acc_done = sem("acc_done")
        stored = sem("stored")

        x_tok = x.rearrange("(t b) c h -> t (b c) h", b=P // C)
        out_tok = out.rearrange("(t b) c h -> t (b c) h", b=P // C)

        LOADS = 6 * G

        def steps(eng, step):
            step(0, 0, 0, first=True)
            step(0, 0, 1)
            with eng.Fori(0, 2) as j:
                step(0, 1, j)
            with eng.Fori(1, SC // 2 - 1) as s:
                with eng.Fori(0, 2) as j:
                    step(s, 0, j)
                with eng.Fori(0, 2) as j:
                    step(s, 1, j)
            with eng.Fori(0, 2) as j:
                step(SC // 2 - 1, 0, j)
            with eng.Fori(0, 2) as j:
                step(SC // 2 - 1, 1, j, last=True)

        def number(s, par, j, q):
            return s * (2 * TG) + j * 2 + (par * TG + q)

        GATE, UP, DOWN = range(3)

        def stored_piece(t, slot, kind, half):
            if kind == DOWN:
                return t.rearrange("p (s n h o m) w -> p s n h o (m w)", s=2, n=3, h=2, o=1)[:, slot, kind, half]
            return t.rearrange("p (s n g c k) w -> p s n c g (k w)", s=2, n=3, c=2, k=KC)[:, slot, kind, half]

        def weight_piece(t, slot, kind, half):
            if kind == DOWN:
                return t.rearrange("p (s n h a k) r -> p s n h a k r", s=2, n=3, h=2, k=KC)[:, slot, kind, half]
            return t.rearrange("p (s n c k g) r -> p s n c g k r", s=2, n=3, c=2, k=KC)[:, slot, kind, half]

        def in_blocks(t):
            return t.rearrange("p (a k r) -> p a k r", k=KC, r=R)

        def piece_number(s, par, j, kind):
            return s * (2 * PIECES) + j * 3 + (par * PIECES + kind)

        block = ctx.enter_context(nc.Block())

        @block.sync
        def _(sp):
            sp.dma_start(who[:, :], itok.rearrange("(o b) -> o b", o=1).to_broadcast([P, B])
                         ).then_inc(who_loaded, 16)

            def load(sc, par):
                rows = bass.ds(sc * (2 * P), 2 * P)
                for g in range(G):
                    to = slice(g * R, (g + 1) * R)
                    for n, (words, scale) in enumerate(((gate_q, gate_s), (up_q, up_s))):
                        blocks = slice(par * BLK + n * BG, par * BLK + (n + 1) * BG)
                        sp.dma_start(
                            packed[to, blocks, :].rearrange("r (b k) w -> r b (k w)", k=KC),
                            words[rows, g * KC * HP:(g + 1) * KC * HP].rearrange("(b r) w -> r b w", r=R)
                        ).then_inc(packed_loaded[par], 16)
                        sp.dma_start(
                            scales[to, blocks].rearrange("r (b k) -> r b k", k=KC),
                            scale[rows, g * KC:(g + 1) * KC].rearrange("(b r) k -> r b k", r=R)
                        ).then_inc(packed_loaded[par], 16)
                    blocks = slice(par * BLK + 2 * BG, par * BLK + 3 * BG)
                    sp.dma_start(
                        packed[to, blocks, :].rearrange("r (b c) w -> r b (c w)", c=2),
                        down_q[:, bass.ds(sc * (2 * G * HP) + g * 2 * HP, 2 * HP)].rearrange("(b r) w -> r b w", r=R)
                    ).then_inc(packed_loaded[par], 16)
                    sp.dma_start(
                        scales[to, blocks].rearrange("r (b c) -> r b c", c=2),
                        down_s[:, bass.ds(sc * (2 * G) + g * 2, 2)].rearrange("(b r) c -> r b c", r=R)
                    ).then_inc(packed_loaded[par], 16)

            load(0, 0)
            for t in range(TG):
                sp.dma_start(acc[:, t * TPG:(t + 1) * TPG, :],
                             x_tok[t * TPG:(t + 1) * TPG].rearrange("t p h -> p t h")
                             ).then_inc(x_loaded[t], 16)
            load(1, 1)
            with sp.Fori(1, SC // 2) as s:
                for par in range(2):
                    sp.wait_ge(w_row_done, s * (2 * PIECES) - (1 - par) * PIECES)
                    load(s * 2 + par, par)
            for t in range(TT):
                sp.wait_ge(acc_done, (SC - 1) * TT + t + 1)
                sp.dma_start(out_tok[t], acc[:, t, :]).then_inc(stored, 16)
            sp.wait_ge(stored, 16 * TT)

        @block.gpsimd
        def _(pool):
            for b in range(P // C):
                nc.gpsimd.iota(chan[b * C:(b + 1) * C, :], [[0, TT]], base=0,
                               channel_multiplier=1).then_inc(chan_made, 1)
            pool.wait_ge(row_made, 2)
            for t in range(TT):
                pool.indirect_dma_start(
                    out=mix[:, t, :], out_offset=None,
                    in_=cond_w.rearrange("s c d -> (s c) d"),
                    in_offset=bass.IndirectOffsetOnAxis(ap=row[:, t:t + 1], axis=0)
                ).then_inc(mix_loaded[t // TPG], 16)

            def weights_lo(s, par, j, kind):
                pool.wait_ge(w_hi_done, piece_number(s, par, j, kind) + 1)
                nc.gpsimd.tensor_tensor(weight_piece(w_lo, par % 2, kind, j), in_blocks(w_col[:, :]),
                                        weight_piece(w_hi, par % 2, kind, j).bitcast(F32),
                                        ALU.subtract).then_inc(w_lo_done, 1)

            for half in range(2):
                for kind in (GATE, UP, DOWN):
                    weights_lo(0, 0, half, kind)

            def step(s, par, j, first=False, last=False):
                for q in range(2):
                    u = number(s, par, j, q)
                    for c in range(2):
                        pool.wait_ge(inter_hi_done, u * 2 + (c + 1))
                        nc.gpsimd.tensor_tensor(inter_lo[:, q, c, :], inter[:, c, :],
                                                inter_hi[:, q, c, :].bitcast(F32),
                                                ALU.subtract).then_inc(inter_lo_done, 1)
                        if not last and (q, c) != (1, 1):
                            weights_lo(s, par + 1, j, 2 * q + c)

            steps(pool, step)

        @block.scalar
        def _(act):
            def turn_x(pair):
                act.wait_ge(x_loaded[pair // 2], 16)
                if pair >= 3:
                    act.wait_ge(h_ready, pair - 2)
                for i in range(2):
                    nc.scalar.activation(
                        work[:, pair % 3, i, :].rearrange("p (k g r) -> p g k r", k=KC, r=R),
                        acc[:, pair * 2 + i, :].rearrange("p (g k r) -> p g k r", k=KC, r=R),
                        ACT.Copy).then_inc(x_turned, 1)

            def weights_hi(s, par, j, kind):
                act.wait_ge(w_col_done, piece_number(s, par, j, kind) + 1)
                nc.scalar.activation(weight_piece(w_hi, par % 2, kind, j), in_blocks(w_col[:, :]),
                                     ACT.Copy).then_inc(w_hi_done, 1)

            def hidden_hi(t):
                act.wait_ge(h_ready, (t + 1) * 2)
                for b in range(P // C):
                    nc.scalar.activation(
                        h_hi[:, :, t * N:(t + 1) * N].rearrange("p k (t b d) -> p b k t d", b=P // C, d=D)[:, b],
                        bank[:, b * KC:(b + 1) * KC, 0:N // 2].rearrange("p k (t d) -> p k t d", d=D),
                        ACT.Copy).then_inc(h_hi_done, 1)

            weights_hi(0, 0, 0, GATE)
            turn_x(0)
            turn_x(1)
            weights_hi(0, 0, 0, UP)
            hidden_hi(0)
            turn_x(2)
            turn_x(3)
            weights_hi(0, 0, 0, DOWN)
            hidden_hi(1)
            turn_x(4)
            turn_x(5)
            weights_hi(0, 0, 1, GATE)
            hidden_hi(2)
            turn_x(6)
            turn_x(7)
            weights_hi(0, 0, 1, UP)
            hidden_hi(3)
            weights_hi(0, 0, 1, DOWN)

            def step(s, par, j, first=False, last=False):
                for q in range(2):
                    u = number(s, par, j, q)
                    for c in range(2):
                        act.wait_ge(gate_ready, u * 2 + (c + 1))
                        nc.scalar.activation(poly[:, c, :], gate_ps[c], ACT.Square).then_inc(square_done, 1)
                        if c == 1 and not last:
                            weights_hi(s, par + 1, j, DOWN if q else GATE)
                        act.wait_ge(arg_done, u * 2 + (c + 1))
                        nc.scalar.activation(tanh[:, c, :], tanh[:, c, :], ACT.Tanh).then_inc(tanh_done, 1)
                        act.wait_ge(inter_done, u * 2 + (c + 1))
                        if not first:
                            act.wait_ge(down_ready, u * TPG - TPG)
                        nc.scalar.activation(inter_hi[:, q, c, :], inter[:, c, :],
                                             ACT.Copy).then_inc(inter_hi_done, 1)
                    if not last and q == 0:
                        weights_hi(s, par + 1, j, UP)

            steps(act, step)

        @block.vector
        def _(dve):
            dve.wait_ge(who_loaded, 16)
            nc.vector.tensor_scalar(held[:, :], who[:, :], 0.0, float(SAMPLES - 1), ALU.max,
                                    ALU.min).then_inc(who_held, 1)
            dve.wait_ge(who_held, 1)
            dve.wait_ge(chan_made, P // C)
            for b in range(P // C):
                half = slice(b * C, (b + 1) * C)
                nc.vector.scalar_tensor_tensor(row[half, :], held[half, :].rearrange("p (t b) -> p b t", b=P // C)[:, b],
                                               float(C), chan[half, :], ALU.mult, ALU.add).then_inc(row_made, 1)

            def unpack(s, par, j, kind):
                dve.wait_ge(packed_loaded[par % 2], (s + (par // 2 + 1)) * (16 * LOADS))
                runs = 1 if kind == DOWN else G
                for t in range(2):
                    nc.vector.tensor_scalar(shifted[:, t, :].rearrange("p (a w) -> p a w", a=runs),
                                            stored_piece(packed, par % 2, kind, j), 28 - 4 * t, 3,
                                            ALU.logical_shift_left,
                                            ALU.arith_shift_right).then_inc(shift_done, 1)

            def mask(s, par, j, kind):
                n = piece_number(s, par, j, kind)
                dve.wait_ge(shift_done, n * 2 + 2)
                nc.vector.tensor_scalar(codes[:, :, :],
                                        shifted[:, :, :].bitcast(U16).rearrange("p t (w e) -> p t w e", e=2)[:, :, :, 1],
                                        CODE_MASK, None, ALU.bitwise_and).then_inc(codes_done, 1)
                runs = 1 if kind == DOWN else G
                nc.vector.tensor_scalar(scale_now[:, :].rearrange("p (a k) -> p a k", a=runs),
                                        stored_piece(scales[:, :].unsqueeze(2), par % 2, kind, j),
                                        CODE_SCALE, None, ALU.mult).then_inc(scale_done, 1)

            def scale(s, par, j, kind):
                n = piece_number(s, par, j, kind)
                dve.wait_ge(codes_done, n + 1)
                dve.wait_ge(scale_done, n + 1)
                nc.vector.tensor_tensor(
                    w_row[:, :].rearrange("p (b i t) -> p t b i", t=2, i=HP),
                    codes[:, :, :].bitcast(F16).rearrange("p t (b i) -> p t b i", i=HP),
                    scale_now[:, :].unsqueeze(1).unsqueeze(3).to_broadcast([P, 2, PB, HP]),
                    ALU.mult).then_inc(w_row_done, 1)

            def turn(s, par, j, kind, follows=True):
                n = piece_number(s, par, j, kind)
                dve.wait_ge(w_row_done, n + 1)
                if follows:
                    dve.wait_ge(w_lo_done, n)
                nc.vector.transpose(w_col[:, :], w_row[:, :]).then_inc(w_col_done, 1)

            def first_piece(half, kind):
                unpack(0, 0, half, kind)
                mask(0, 0, half, kind)
                scale(0, 0, half, kind)
                turn(0, 0, half, kind, (half, kind) != (0, GATE))

            def hidden_lo(t):
                dve.wait_ge(h_hi_done, (t + 1) * 2)
                for b in range(P // C):
                    to = [v[:, :, t * N:(t + 1) * N].rearrange("p k (t b d) -> p b k t d", b=P // C, d=D)[:, b]
                          for v in (h_lo, h_hi)]
                    nc.vector.tensor_tensor(
                        to[0], bank[:, b * KC:(b + 1) * KC, 0:N // 2].rearrange("p k (t d) -> p k t d", d=D),
                        to[1].bitcast(F32), ALU.subtract).then_inc(h_lo_done, 1)

            first_piece(0, GATE)
            first_piece(0, UP)
            hidden_lo(0)
            first_piece(0, DOWN)
            hidden_lo(1)
            first_piece(1, GATE)
            hidden_lo(2)
            first_piece(1, UP)
            hidden_lo(3)
            first_piece(1, DOWN)

            def gelu(n, c, follows):
                dve.wait_ge(square_done, n)
                nc.vector.tensor_scalar(poly[:, c, :], poly[:, c, :], GELU_C * GELU_A, GELU_C,
                                        ALU.mult, ALU.add).then_inc(poly_done, 1)
                dve.wait_ge(poly_done, n)
                nc.vector.tensor_tensor(tanh[:, c, :], poly[:, c, :], gate_ps[c],
                                        ALU.mult).then_inc(arg_done, 1)
                dve.wait_ge(tanh_done, n)
                nc.vector.scalar_tensor_tensor(tanh[:, c, :], tanh[:, c, :], 1.0, gate_ps[c],
                                               ALU.add, ALU.mult).then_inc(gelu_done, 1)
                dve.wait_ge(gelu_done, n)
                dve.wait_ge(up_ready, n)
                if follows:
                    dve.wait_ge(inter_lo_done, n - 2)
                nc.vector.scalar_tensor_tensor(inter[:, c, :], tanh[:, c, :], 0.5, up_ps[c],
                                               ALU.mult, ALU.mult).then_inc(inter_done, 1)

            def add_down(done, group, half):
                for i in (2 * half, 2 * half + 1):
                    dve.wait_ge(down_ready, done + (i + 1))
                    tile = acc[:, bass.ds(group * TPG + i, 1), :].rearrange("p o h -> p (o h)")
                    nc.vector.tensor_tensor(tile, bank[:, 4 + i, :], tile, ALU.add).then_inc(acc_done, 1)

            def step(s, par, j, first=False, last=False):
                for q in range(2):
                    u = number(s, par, j, q)
                    group = j * 2 if q else j * -2 + 3
                    follows = not (first and q == 0)
                    kind = DOWN if q else GATE
                    if not last:
                        unpack(s, par + 1, j, kind)
                    gelu(u * 2 + 1, 0, follows)
                    if not last:
                        mask(s, par + 1, j, kind)
                    if follows:
                        add_down(u * TPG - TPG, group, 0)
                    if not last:
                        scale(s, par + 1, j, kind)
                        turn(s, par + 1, j, kind)
                        if q == 0:
                            unpack(s, par + 1, j, UP)
                    gelu(u * 2 + 2, 1, follows)
                    if not last and q == 0:
                        mask(s, par + 1, j, UP)
                        scale(s, par + 1, j, UP)
                        turn(s, par + 1, j, UP)
                    if follows:
                        add_down(u * TPG - TPG, group, 1)

            steps(dve, step)
            add_down((SC * TG - 1) * TPG, TG - 1, 0)
            add_down((SC * TG - 1) * TPG, TG - 1, 1)

        @block.tensor
        def _(pe):
            for t in range(TG):
                pe.wait_ge(mix_loaded[t], 16 * TPG)
                if t:
                    pe.wait_ge(h_lo_done, t * 2)
                for i in range(TPG):
                    pair = t * 2 + i // 2
                    pe.wait_ge(x_turned, pair * 2 + i % 2 + 1)
                    for kc in range(KC):
                        for b in range(P // C):
                            rows = slice(b * C, (b + 1) * C)
                            last = nc.tensor.matmul(
                                bank[:, b * KC + kc, i * D:(i + 1) * D],
                                work[rows, pair % 3, i % 2, kc * P:(kc + 1) * P],
                                mix[rows, t * TPG + i, :], start=True, stop=True)
                    if i % 2:
                        last.then_inc(h_ready, 1)
            pe.wait_ge(h_lo_done, TG * 2)

            def thrice(ps, terms):
                for n, (a_hi, a_lo, b_hi, b_lo) in enumerate(terms):
                    nc.tensor.matmul(ps, a_hi, b_hi, start=(n == 0), stop=False)
                    nc.tensor.matmul(ps, a_hi, b_lo, start=False, stop=False)
                    last = nc.tensor.matmul(ps, a_lo, b_hi, start=False, stop=(n == len(terms) - 1))
                return last

            def gate_up(par, group, c):
                tokens = bass.ds(group * N, N)
                for n, (ps, ready) in enumerate(((gate_ps[c], gate_ready), (up_ps[c], up_ready))):
                    w = [v[:, :, :].rearrange("p (s n c k g) r -> p s n c k (g r)", s=2, n=3, c=2,
                                              k=KC)[:, par, n, c] for v in (w_hi, w_lo)]
                    thrice(ps, [(w[0][:, kc], w[1][:, kc], h_hi[:, kc, tokens], h_lo[:, kc, tokens])
                                for kc in range(KC)]).then_inc(ready, 1)

            def down(slot, q, half, freed):
                w = [v[:, :, :].rearrange("p (s n b c) r -> p s n c b r", s=2, n=3, c=2)[:, slot, DOWN]
                     for v in (w_hi, w_lo)]
                for i in (2 * half, 2 * half + 1):
                    if freed is not None:
                        pe.wait_ge(acc_done, freed + (i + 1))
                    tile = slice(i * P, (i + 1) * P)
                    thrice(bank[:, 4 + i, :],
                           [(inter_hi[:, q, c, tile], inter_lo[:, q, c, tile], w[0][:, c], w[1][:, c])
                            for c in range(2)]).then_inc(down_ready, 1)

            def step(s, par, j, first=False, last=False):
                for q in range(2):
                    u = number(s, par, j, q)
                    slot = par if q else (j if par else j * -1 + 1)
                    freed = None if first else u * TPG - 2 * TPG
                    follows = not (first and q == 0)
                    pe.wait_ge(w_lo_done, s * (2 * PIECES) + (par * PIECES + 2))
                    if follows:
                        pe.wait_ge(inter_done, u * 2 - 1)
                    gate_up(par, j * 2 + q, 0)
                    if follows:
                        pe.wait_ge(inter_lo_done, u * 2)
                        if q:
                            pe.wait_ge(w_lo_done, s * (2 * PIECES) + (par + 1) * PIECES)
                        down(slot, 1 - q, 0, freed)
                        pe.wait_ge(inter_done, u * 2)
                    pe.wait_ge(w_lo_done, s * (2 * PIECES) + (par * PIECES + 5))
                    gate_up(par, j * 2 + q, 1)
                    if follows:
                        down(slot, 1 - q, 1, freed)

            steps(pe, step)
            pe.wait_ge(inter_lo_done, SC * TG * 2)
            down(1, 1, 0, (SC * TG - 2) * TPG)
            down(1, 1, 1, (SC * TG - 2) * TPG)


_INS = ['x', 'itok_B_1_198', 'L0_cond_weights', 'L0_ffn_gate_W_packed', 'L0_ffn_gate_scales',
        'L0_ffn_up_W_packed', 'L0_ffn_up_scales', 'L0_ffn_down_W_packed', 'L0_ffn_down_scales']


def kernel(**inputs):
    import numpy as np
    import concourse.bacc as bacc
    from concourse.bass_utils import run_bass_kernel_spmd as run

    nc = bacc.Bacc("TRN2", target_bir_lowering=False, num_devices=1)
    arrays, args = {}, []
    for name in _INS:
        a = np.ascontiguousarray(inputs[name])
        arrays[name] = a
        args.append(nc.dram_tensor(name, a.shape, mybir.dt.from_np(a.dtype), kind="ExternalInput").ap())
    out = nc.dram_tensor("out", arrays['x'].shape, F32, kind="ExternalOutput").ap()
    build(nc, *args, out)
    return run(nc, [arrays], core_ids=[0]).results[0]["out"]
```

```python
from contextlib import ExitStack

import concourse.bass as bass
from concourse import mybir

F32 = mybir.dt.float32
F16 = mybir.dt.float16
I32 = mybir.dt.int32
U16 = mybir.dt.uint16
U32 = mybir.dt.uint32
ALU = mybir.AluOpType
ACT = mybir.ActivationFunctionType
AX = mybir.AxisListType
MAX = bass.bass_isa.ReduceOp.max

P = 128
G = 4
R = 32
N = 512
LO_UP = 2.0 ** 11
H_EXP = 14
W_EXP = 12
INTER_EXP = -13
LEAST = 2.0 ** -100
EXP_BITS = 0x7F800000
GELU_C = 0.7978845608028654
GELU_A = 0.044715
CODE_MASK = 0x8E00
CODE_EXP = 14


def build(nc, x, itok, cond_w, gate_q, gate_s, up_q, up_s, down_q, down_s, out):
    B, C, H = x.shape
    SAMPLES, _, D = cond_w.shape
    MLP = gate_q.shape[0]
    TOK = B * D
    TG = TOK // N
    TT = TOK // P
    TPG = N // P
    KC = H // P
    SC = MLP // (2 * P)
    BG = 2 * G * KC
    BLK = 3 * BG
    PIECES = 6
    PB = BLK // PIECES
    PW = PB * R
    RING = TT // TPG
    HP = R // 2
    assert C == 64 and D == 64 and BG == 2 * H // R and TG == 4 and SC % 2 == 0

    ctx = ExitStack()
    with ctx:
        def sb(name, shape, dt):
            return ctx.enter_context(nc.sbuf_tensor(name, shape, dt))

        def sem(name):
            return ctx.enter_context(nc.semaphore(name))

        acc = sb("acc", [P, TT, H], F32)
        h_hi = sb("h_hi", [P, KC, TOK], F16)
        h_lo = sb("h_lo", [P, KC, TOK], F16)
        w_hi = sb("w_hi", [P, 2 * BLK, R], F16)
        w_lo = sb("w_lo", [P, 2 * BLK, R], F16)
        w_down_small = sb("w_down_small", [P, 2 * BG, R], F16)
        inter_hi = sb("inter_hi", [P, 2, 2, N], F16)
        inter_lo = sb("inter_lo", [P, 2, 2, N], F16)
        packed = sb("packed", [P, 2 * BLK, HP], I32)
        scales = sb("scales", [P, 2 * BLK], F32)
        shifted = sb("shifted", [P, 2, PB * HP], I32)
        codes = sb("codes", [P, 2, PB * HP], U16)
        w_row = sb("w_row", [P, PW], F32)
        w_col = sb("w_col", [P, 3, PW], F32)
        scale_now = sb("scale_now", [P, PB], F32)
        poly = sb("poly", [P, 2, N], F32)
        tanh = sb("tanh", [P, 2, N], F32)
        inter = sb("inter", [P, 2, N], F32)
        x_col = sb("x_col", [P, RING, 2, H], F32)
        h_full = sb("h_full", [P, KC, TOK], F32)
        all_scales = sb("all_scales", [P, 3, MLP * (H // R) // P], F32)
        w_max = sb("w_max", [P, 3], F32)
        w_top = sb("w_top", [P, 3], F32)
        w_factor = sb("w_factor", [P, 3], F32)
        h_max = sb("h_max", [P, TT // 2], F32)
        h_most = sb("h_most", [P, 1], F32)
        h_top = sb("h_top", [P, 1], F32)
        h_factor = sb("h_factor", [P, 1], F32)
        gate_unit = sb("gate_unit", [P, 1], F32)
        down_unit = sb("down_unit", [P, 1], F32)
        h_square = sb("h_square", [P, 1], F32)
        w_product = sb("w_product", [P, 1], F32)
        mix = sb("mix", [P, TT, D], F32)
        mix_pair = sb("mix_pair", [P, TT, P // C, D], F32)
        who = sb("who", [P, B], I32)
        held = sb("held", [P, B], I32)
        chan = sb("chan", [P, TT], I32)
        row = sb("row", [P, TT], U32)
        bank = ctx.enter_context(nc.psum_tensor("bank", [P, 8, N], F32))
        gate_ps = [bank[:, 0, :], bank[:, 2, :]]
        up_ps = [bank[:, 1, :], bank[:, 3, :]]

        x_loaded = [sem(f"x_loaded{t}") for t in range(TT // 2)]
        who_loaded = sem("who_loaded")
        chan_made = sem("chan_made")
        who_held = sem("who_held")
        row_made = sem("row_made")
        scales_loaded = sem("scales_loaded")
        w_max_done = sem("w_max_done")
        w_top_done = sem("w_top_done")
        w_power_done = sem("w_power_done")
        w_factor_done = sem("w_factor_done")
        h_full_done = sem("h_full_done")
        h_max_done = sem("h_max_done")
        h_most_done = sem("h_most_done")
        h_top_done = sem("h_top_done")
        h_power_done = sem("h_power_done")
        h_factor_done = sem("h_factor_done")
        unit_done = sem("unit_done")
        units_ready = sem("units_ready")
        w_small_done = sem("w_small_done")
        mix_cleared = sem("mix_cleared")
        mix_placed = sem("mix_placed")
        mix_loaded = [sem(f"mix_loaded{t}") for t in range(TT // 2)]
        packed_loaded = [[sem(f"packed_loaded{p}{k}") for k in range(3)] for p in range(2)]
        x_turned = sem("x_turned")
        h_ready = sem("h_ready")
        h_hi_done = sem("h_hi_done")
        h_scaled_done = sem("h_scaled_done")
        h_lo_done = sem("h_lo_done")
        shift_done = sem("shift_done")
        codes_done = sem("codes_done")
        scale_done = sem("scale_done")
        w_row_done = sem("w_row_done")
        w_col_done = sem("w_col_done")
        w_hi_done = sem("w_hi_done")
        w_lo_done = sem("w_lo_done")
        gate_ready = sem("gate_ready")
        up_ready = sem("up_ready")
        square_done = sem("square_done")
        poly_done = sem("poly_done")
        arg_done = sem("arg_done")
        tanh_done = sem("tanh_done")
        gelu_done = sem("gelu_done")
        inter_done = sem("inter_done")
        inter_hi_done = sem("inter_hi_done")
        inter_lo_done = sem("inter_lo_done")
        down_ready = sem("down_ready")
        acc_done = sem("acc_done")
        stored = sem("stored")

        x_tok = x.rearrange("(t b) c h -> t (b c) h", b=P // C)
        out_tok = out.rearrange("(t b) c h -> t (b c) h", b=P // C)

        LOADS = 2 * G

        def steps(eng, step):
            step(0, 0, 0, first=True)
            step(0, 0, 1, second=True)
            with eng.Fori(0, 2) as j:
                step(0, 1, j)
            with eng.Fori(1, SC // 2 - 1) as s:
                with eng.Fori(0, 2) as j:
                    step(s, 0, j)
                with eng.Fori(0, 2) as j:
                    step(s, 1, j)
            with eng.Fori(0, 2) as j:
                step(SC // 2 - 1, 0, j)
            with eng.Fori(0, 2) as j:
                step(SC // 2 - 1, 1, j, last=True)

        def number(s, par, j, q):
            return s * (2 * TG) + j * 2 + (par * TG + q)

        GATE, UP, DOWN = range(3)

        def stored_piece(t, slot, kind, half):
            if kind == DOWN:
                return t.rearrange("p (s n h o m) w -> p s n h o (m w)", s=2, n=3, h=2, o=1)[:, slot, kind, half]
            return t.rearrange("p (s n g c k) w -> p s n c g (k w)", s=2, n=3, c=2, k=KC)[:, slot, kind, half]

        def weight_piece(t, slot, kind, half):
            if kind == DOWN:
                return t.rearrange("p (s n h a k) r -> p s n h a k r", s=2, n=3, h=2, k=KC)[:, slot, kind, half]
            return t.rearrange("p (s n c k g) r -> p s n c g k r", s=2, n=3, c=2, k=KC)[:, slot, kind, half]

        def in_blocks(t):
            return t.rearrange("p (a k r) -> p a k r", k=KC, r=R)

        def piece(s, par, j, kind):
            return s * (2 * PIECES) + j * 3 + (par * PIECES + kind), par % 2, kind, j

        FIRST = [(0, 0, GATE, 0), (1, 0, UP, 0), (2, 0, GATE, 1), (3, 0, UP, 1),
                 (4, 0, DOWN, 0), (5, 0, DOWN, 1)]

        block = ctx.enter_context(nc.Block())

        @block.sync
        def _(sp):
            sp.dma_start(who[:, :], itok.rearrange("(o b) -> o b", o=1).to_broadcast([P, B])
                         ).then_inc(who_loaded, 16)

            def load(sc, par, kind):
                words, scale = ((gate_q, gate_s), (up_q, up_s), (down_q, down_s))[kind]
                rows = bass.ds(sc * (2 * P), 2 * P)
                blocks = slice(par * BLK + kind * BG, par * BLK + (kind + 1) * BG)
                run = 2 if kind == DOWN else KC
                for g in range(G):
                    to = slice(g * R, (g + 1) * R)
                    if kind == DOWN:
                        w_from = words[:, bass.ds(sc * (2 * G * HP) + g * 2 * HP, 2 * HP)]
                        s_from = scale[:, bass.ds(sc * (2 * G) + g * 2, 2)]
                    else:
                        w_from = words[rows, g * KC * HP:(g + 1) * KC * HP]
                        s_from = scale[rows, g * KC:(g + 1) * KC]
                    sp.dma_start(packed[to, blocks, :].rearrange("r (b k) w -> r b (k w)", k=run),
                                 w_from.rearrange("(b r) w -> r b w", r=R)).then_inc(packed_loaded[par][kind], 16)
                    sp.dma_start(scales[to, blocks].rearrange("r (b k) -> r b k", k=run),
                                 s_from.rearrange("(b r) k -> r b k", r=R)).then_inc(packed_loaded[par][kind], 16)

            def load_x(pair):
                tiles = slice(pair * 2, pair * 2 + 2)
                sp.dma_start(acc[:, tiles, :], x_tok[tiles].rearrange("t p h -> p t h")
                             ).then_inc(x_loaded[pair], 16)

            load_x(0)
            load_x(1)
            load_x(2)
            load(0, 0, GATE)
            load_x(3)
            load(0, 0, UP)
            for pair in range(4, TT // 2):
                sp.wait_ge(x_turned, (pair - 2) * 2)
                load_x(pair)
            load(0, 0, DOWN)
            for kind in (GATE, UP, DOWN):
                load(1, 1, kind)
            with sp.Fori(1, SC // 2) as s:
                for par in range(2):
                    sp.wait_ge(w_row_done, s * (2 * PIECES) - (1 - par) * PIECES)
                    for kind in (GATE, UP, DOWN):
                        load(s * 2 + par, par, kind)
            for t in range(TT):
                sp.wait_ge(acc_done, (SC - 1) * TT + t + 1)
                sp.dma_start(out_tok[t], acc[:, t, :]).then_inc(stored, 16)
            sp.wait_ge(stored, 16 * TT)

        @block.gpsimd
        def _(pool):
            for b in range(P // C):
                nc.gpsimd.iota(chan[b * C:(b + 1) * C, :], [[0, TT]], base=0,
                               channel_multiplier=1).then_inc(chan_made, 1)
            pool.wait_ge(row_made, 2)
            def gather(t):
                pool.indirect_dma_start(
                    out=mix[:, t, :], out_offset=None,
                    in_=cond_w.rearrange("s c d -> (s c) d"),
                    in_offset=bass.IndirectOffsetOnAxis(ap=row[:, t:t + 1], axis=0)
                ).then_inc(mix_loaded[t // 2], 16)

            def weights_lo(n, slot, kind, half):
                pool.wait_ge(w_hi_done, n + 1)
                nc.gpsimd.tensor_tensor(weight_piece(w_lo, slot, kind, half), in_blocks(w_col[:, kind, :]),
                                        weight_piece(w_hi, slot, kind, half),
                                        ALU.subtract).then_inc(w_lo_done, 1)

            def hidden_lo(t, kc):
                pool.wait_ge(h_scaled_done, (t - 1) * KC + kc + 1)
                part = (slice(None), kc, slice(t * N, (t + 1) * N))
                nc.gpsimd.tensor_tensor(h_lo[part], h_full[part], h_hi[part],
                                        ALU.subtract).then_inc(h_lo_done, 1)

            for t in range(7):
                gather(t)
            pool.wait_ge(w_max_done, 1)
            pool.partition_all_reduce(w_top[:, :], w_max[:, :], P, MAX).then_inc(w_top_done, 1)
            for t in range(7, TT):
                gather(t)
            weights_lo(*FIRST[0])
            weights_lo(*FIRST[1])
            pool.wait_ge(h_most_done, 1)
            pool.partition_all_reduce(h_top[:, :], h_most[:, :], P, MAX).then_inc(h_top_done, 1)
            pool.wait_ge(h_lo_done, KC)
            hidden_lo(1, 0)
            weights_lo(*FIRST[2])
            hidden_lo(1, 1)
            hidden_lo(1, 2)
            weights_lo(*FIRST[3])
            weights_lo(*FIRST[4])
            hidden_lo(1, 3)
            hidden_lo(2, 0)
            weights_lo(*FIRST[5])
            for kc in (1, 2, 3):
                hidden_lo(2, kc)
            for kc in range(KC):
                hidden_lo(3, kc)

            def step(s, par, j, first=False, second=False, last=False):
                if not last:
                    for kind in (GATE, UP, DOWN):
                        weights_lo(*piece(s, par + 1, j, kind))

            steps(pool, step)

        @block.scalar
        def _(act):
            for kind, scale in enumerate((gate_s, up_s, down_s)):
                act.dma_start(all_scales[:, kind, :],
                              scale.rearrange("(p n) k -> p (n k)", p=P)).then_inc(scales_loaded, 16)

            def turn_x(pair):
                act.wait_ge(x_loaded[pair], 16)
                if pair >= RING:
                    act.wait_ge(h_ready, pair - RING + 1)
                for i in range(2):
                    nc.scalar.activation(
                        x_col[:, pair % RING, i, :].rearrange("p (k g r) -> p g k r", k=KC, r=R),
                        acc[:, pair * 2 + i, :].rearrange("p (g k r) -> p g k r", k=KC, r=R),
                        ACT.Copy).then_inc(x_turned, 1)

            def keep_h(pair):
                act.wait_ge(h_ready, pair + 1)
                nc.scalar.activation(
                    h_full[:, :, pair * 2 * P:(pair + 1) * 2 * P].rearrange("p k (i t) -> p i k t", i=2),
                    bank[:, pair % 4 * 2:pair % 4 * 2 + 2, :].rearrange("p i (k t) -> p i k t", k=KC),
                    ACT.Copy).then_inc(h_full_done, 1)

            def weights_hi(n, slot, kind, half):
                act.wait_ge(w_col_done, n + 1)
                hi = weight_piece(w_hi, slot, kind, half)
                nc.scalar.activation(hi, in_blocks(w_col[:, kind, :]), ACT.Copy).then_inc(w_hi_done, 1)
                if kind == DOWN:
                    act.wait_ge(w_hi_done, n + 1)
                    nc.scalar.activation(
                        w_down_small[:, :, :].rearrange("p (s h a k) r -> p s h a k r", s=2, h=2, k=KC)[:, slot, half],
                        hi, ACT.Copy, scale=1.0 / LO_UP).then_inc(w_small_done, 1)

            def hidden_hi(t, kc):
                part = (slice(None), kc, slice(t * N, (t + 1) * N))
                nc.scalar.activation(h_hi[part], h_full[part], ACT.Copy,
                                     scale=h_factor[:, :]).then_inc(h_hi_done, 1)
                if t:
                    act.wait_ge(h_hi_done, t * KC + kc + 1)
                    nc.scalar.activation(h_full[part], h_full[part], ACT.Copy,
                                         scale=h_factor[:, :]).then_inc(h_scaled_done, 1)

            for pair in range(RING):
                turn_x(pair)
            for pair in range(TT // 2):
                keep_h(pair)
                if pair + RING < TT // 2:
                    turn_x(pair + RING)
                if pair in (2, 4):
                    weights_hi(*FIRST[pair // 2 - 1])
            act.wait_ge(h_factor_done, 1)
            act.wait_ge(h_full_done, TT // 2)
            for kc in range(KC):
                hidden_hi(0, kc)
            hidden_hi(1, 0)
            weights_hi(*FIRST[2])
            hidden_hi(1, 1)
            hidden_hi(1, 2)
            weights_hi(*FIRST[3])
            left = {(0, 0): ([(1, 3)], [(2, 0)]), (0, 1): ([(2, 1)], [(2, 2), (2, 3)]),
                    (1, 0): ([(3, 0)], [(3, 1)]), (1, 1): ([(3, 2)], [(3, 3)])}
            act.wait_ge(units_ready, 1)

            def step(s, par, j, first=False, second=False, last=False):
                for q in range(2):
                    u = number(s, par, j, q)
                    for c in range(2):
                        act.wait_ge(gate_ready, u * 2 + (c + 1))
                        nc.scalar.activation(poly[:, c, :], gate_ps[c], ACT.Square,
                                             scale=gate_unit[:, :]).then_inc(square_done, 1)
                        if first and q == 0:
                            weights_hi(*FIRST[4 + c])
                        elif first:
                            weights_hi(*piece(s, par + 1, j, UP if c else GATE))
                        elif c == 1 and not last:
                            weights_hi(*piece(s, par + 1, j, DOWN if q else GATE))
                        act.wait_ge(arg_done, u * 2 + (c + 1))
                        nc.scalar.activation(tanh[:, c, :], tanh[:, c, :], ACT.Tanh).then_inc(tanh_done, 1)
                        if first:
                            for chunk in left[q, c][0]:
                                hidden_hi(*chunk)
                        act.wait_ge(inter_done, u * 2 + (c + 1))
                        if not first:
                            act.wait_ge(down_ready, u * TPG - TPG)
                        nc.scalar.activation(inter_hi[:, q, c, :], inter[:, c, :], ACT.Copy,
                                             scale=1.0 / LO_UP).then_inc(inter_hi_done, 1)
                        if first:
                            for chunk in left[q, c][1]:
                                hidden_hi(*chunk)
                    if first and q:
                        weights_hi(*piece(s, par + 1, j, DOWN))
                    elif not (first or last) and q == 0:
                        weights_hi(*piece(s, par + 1, j, UP))

            steps(act, step)

        @block.vector
        def _(dve):
            nc.vector.memset(mix_pair[:, :, :, :], 0.0).then_inc(mix_cleared, 1)
            dve.wait_ge(who_loaded, 16)
            nc.vector.tensor_scalar(held[:, :], who[:, :], 0.0, float(SAMPLES - 1), ALU.max,
                                    ALU.min).then_inc(who_held, 1)
            dve.wait_ge(who_held, 1)
            dve.wait_ge(chan_made, P // C)
            for b in range(P // C):
                half = slice(b * C, (b + 1) * C)
                nc.vector.scalar_tensor_tensor(row[half, :], held[half, :].rearrange("p (t b) -> p b t", b=P // C)[:, b],
                                               float(C), chan[half, :], ALU.mult, ALU.add).then_inc(row_made, 1)

            def unpack(n, slot, kind, half, loads):
                dve.wait_ge(packed_loaded[slot][kind], loads * (16 * LOADS))
                runs = 1 if kind == DOWN else G
                for t in range(2):
                    nc.vector.tensor_scalar(shifted[:, t, :].rearrange("p (a w) -> p a w", a=runs),
                                            stored_piece(packed, slot, kind, half), 28 - 4 * t, 3,
                                            ALU.logical_shift_left,
                                            ALU.arith_shift_right).then_inc(shift_done, 1)

            def mask(n, slot, kind, half):
                dve.wait_ge(shift_done, n * 2 + 2)
                nc.vector.tensor_scalar(codes[:, :, :],
                                        shifted[:, :, :].bitcast(U16).rearrange("p t (w e) -> p t w e", e=2)[:, :, :, 1],
                                        CODE_MASK, None, ALU.bitwise_and).then_inc(codes_done, 1)
                runs = 1 if kind == DOWN else G
                nc.vector.tensor_scalar(scale_now[:, :].rearrange("p (a k) -> p a k", a=runs),
                                        stored_piece(scales[:, :].unsqueeze(2), slot, kind, half),
                                        w_factor[:, kind:kind + 1], None, ALU.mult).then_inc(scale_done, 1)

            def scale(n, slot, kind, half):
                dve.wait_ge(codes_done, n + 1)
                dve.wait_ge(scale_done, n + 1)
                nc.vector.tensor_tensor(
                    w_row[:, :].rearrange("p (b i t) -> p t b i", t=2, i=HP),
                    codes[:, :, :].bitcast(F16).rearrange("p t (b i) -> p t b i", i=HP),
                    scale_now[:, :].unsqueeze(1).unsqueeze(3).to_broadcast([P, 2, PB, HP]),
                    ALU.mult).then_inc(w_row_done, 1)

            def turn(n, slot, kind, half, before=3):
                dve.wait_ge(w_row_done, n + 1)
                if before:
                    dve.wait_ge(w_lo_done, n - (before - 1))
                nc.vector.transpose(w_col[:, kind, :], w_row[:, :]).then_inc(w_col_done, 1)

            def first_piece(p, before=0):
                unpack(*p, 1)
                mask(*p)
                scale(*p)
                turn(*p, before)

            def largest_h(pair):
                dve.wait_ge(h_full_done, pair + 1)
                nc.vector.tensor_reduce(h_max[:, pair:pair + 1], h_full[:, :, pair * 2 * P:(pair + 1) * 2 * P],
                                        AX.XY, ALU.max, apply_absolute_value=True).then_inc(h_max_done, 1)

            def power(top, done):
                nc.vector.tensor_scalar(top[:, :], top[:, :], LEAST, None, ALU.max).then_inc(done, 1)
                dve.wait_ge(done, 1)
                bits = top[:, :].bitcast(I32)
                nc.vector.tensor_scalar(bits, bits, EXP_BITS, None, ALU.bitwise_and).then_inc(done, 1)
                dve.wait_ge(done, 2)

            def inverse(out, top, exp, done):
                nc.vector.tensor_scalar(out[:, :].bitcast(I32), top[:, :].bitcast(I32), -1.0,
                                        float((254 + exp) << 23), ALU.mult, ALU.add).then_inc(done, 1)

            def hidden_lo():
                for kc in range(KC):
                    part = (slice(None), kc, slice(0, N))
                    dve.wait_ge(h_hi_done, kc + 1)
                    nc.vector.scalar_tensor_tensor(h_lo[part], h_full[part], h_factor[:, :], h_hi[part],
                                                   ALU.mult, ALU.subtract).then_inc(h_lo_done, 1)

            def place_mix(pair):
                dve.wait_ge(mix_loaded[pair], 16 * 2)
                for b in range(P // C):
                    part = (slice(b * C, (b + 1) * C), slice(pair * 2, pair * 2 + 2))
                    nc.vector.tensor_copy(mix_pair[part + (b,)], mix[part]).then_inc(mix_placed, 1)

            dve.wait_ge(mix_cleared, 1)
            dve.wait_ge(scales_loaded, 16 * 3)
            nc.vector.tensor_reduce(w_max[:, :], all_scales[:, :, :], AX.X, ALU.max,
                                    apply_absolute_value=True).then_inc(w_max_done, 1)
            place_mix(0)
            dve.wait_ge(w_top_done, 1)
            power(w_top, w_power_done)
            inverse(w_factor, w_top, W_EXP + CODE_EXP, w_factor_done)
            dve.wait_ge(w_factor_done, 1)
            unpack(*FIRST[0], 1)
            mask(*FIRST[0])
            scale(*FIRST[0])
            place_mix(1)
            turn(*FIRST[0], 0)
            place_mix(2)
            first_piece(FIRST[1])
            for pair in range(3, TT // 2):
                place_mix(pair)
                if pair == 6:
                    unpack(*FIRST[2], 1)
                    mask(*FIRST[2])
                if pair == 7:
                    scale(*FIRST[2])
                largest_h(pair - 3)
            for pair in range(TT // 2 - 3, TT // 2):
                largest_h(pair)
            dve.wait_ge(h_max_done, TT // 2)
            nc.vector.tensor_reduce(h_most[:, :], h_max[:, :], AX.X, ALU.max).then_inc(h_most_done, 1)
            nc.vector.tensor_scalar(w_product[:, :], w_top[:, 0:1], w_top[:, 1:2], w_top[:, 2:3],
                                    ALU.mult, ALU.mult).then_inc(unit_done, 1)
            turn(*FIRST[2], 2)
            dve.wait_ge(h_top_done, 1)
            power(h_top, h_power_done)
            inverse(h_factor, h_top, H_EXP, h_factor_done)
            nc.vector.tensor_scalar(gate_unit[:, :], h_top[:, :], w_top[:, 0:1], 2.0 ** -(H_EXP + W_EXP),
                                    ALU.mult, ALU.mult).then_inc(unit_done, 1)
            nc.vector.tensor_scalar(h_square[:, :], h_top[:, :], h_top[:, :], 2.0 ** -(INTER_EXP + W_EXP),
                                    ALU.mult, ALU.mult).then_inc(unit_done, 1)
            dve.wait_ge(unit_done, 3)
            nc.vector.tensor_tensor(down_unit[:, :], h_square[:, :], w_product[:, :], ALU.mult).then_inc(units_ready, 1)
            unpack(*FIRST[3], 1)
            dve.wait_ge(h_factor_done, 1)
            dve.wait_ge(units_ready, 1)
            hidden_lo()
            mask(*FIRST[3])
            scale(*FIRST[3])
            turn(*FIRST[3], 2)
            first_piece(FIRST[4])

            def gelu(n, c):
                dve.wait_ge(square_done, n)
                nc.vector.tensor_scalar(poly[:, c, :], poly[:, c, :], GELU_C * GELU_A, GELU_C,
                                        ALU.mult, ALU.add).then_inc(poly_done, 1)
                dve.wait_ge(poly_done, n)
                nc.vector.scalar_tensor_tensor(tanh[:, c, :], gate_ps[c], gate_unit[:, :], poly[:, c, :],
                                               ALU.mult, ALU.mult).then_inc(arg_done, 1)
                dve.wait_ge(tanh_done, n)
                nc.vector.scalar_tensor_tensor(tanh[:, c, :], tanh[:, c, :], 1.0, gate_ps[c],
                                               ALU.add, ALU.mult).then_inc(gelu_done, 1)
                dve.wait_ge(gelu_done, n)
                dve.wait_ge(up_ready, n)
                nc.vector.scalar_tensor_tensor(
                    inter[:, c, :], tanh[:, c, :], 0.5 * LO_UP * 2.0 ** (INTER_EXP - 2 * (H_EXP + W_EXP)),
                    up_ps[c], ALU.mult, ALU.mult).then_inc(inter_done, 1)

            def split_lo(n, q, c):
                dve.wait_ge(inter_hi_done, n)
                nc.vector.scalar_tensor_tensor(inter_lo[:, q, c, :], inter_hi[:, q, c, :], -LO_UP, inter[:, c, :],
                                               ALU.mult, ALU.add).then_inc(inter_lo_done, 1)

            def add_down(done, group, half):
                for i in (2 * half, 2 * half + 1):
                    dve.wait_ge(down_ready, done + (i + 1))
                    tile = acc[:, bass.ds(group * TPG + i, 1), :].rearrange("p o h -> p (o h)")
                    nc.vector.scalar_tensor_tensor(tile, bank[:, 4 + i, :], down_unit[:, :], tile,
                                                   ALU.mult, ALU.add).then_inc(acc_done, 1)

            def step(s, par, j, first=False, second=False, last=False):
                for q in range(2):
                    u = number(s, par, j, q)
                    group = j * 2 if q else j * -2 + 3
                    p, p_up = piece(s, par + 1, j, DOWN if q else GATE), piece(s, par + 1, j, UP)
                    loads = s + ((par + 1) // 2 + 1)
                    if first:
                        gelu(u * 2 + 1, 0)
                        split_lo(u * 2 + 1, q, 0)
                        if q:
                            add_down(u * TPG - TPG, group, 0)
                            first_piece(piece(s, par + 1, j, UP), 3)
                        else:
                            first_piece(FIRST[5], 1)
                        gelu(u * 2 + 2, 1)
                        split_lo(u * 2 + 2, q, 1)
                        if q:
                            first_piece(piece(s, par + 1, j, DOWN), 3)
                            add_down(u * TPG - TPG, group, 1)
                        else:
                            first_piece(piece(s, par + 1, j, GATE), 3)
                        continue
                    if not last:
                        unpack(*p, loads)
                    gelu(u * 2 + 1, 0)
                    if not last:
                        mask(*p)
                    split_lo(u * 2 + 1, q, 0)
                    add_down(u * TPG - TPG, group, 0)
                    if not last:
                        scale(*p)
                        turn(*p)
                        if q == 0:
                            unpack(*p_up, loads)
                    gelu(u * 2 + 2, 1)
                    if not last and q == 0:
                        mask(*p_up)
                    split_lo(u * 2 + 2, q, 1)
                    if not last and q == 0:
                        scale(*p_up)
                        turn(*p_up)
                    add_down(u * TPG - TPG, group, 1)

            steps(dve, step)
            add_down((SC * TG - 1) * TPG, TG - 1, 0)
            add_down((SC * TG - 1) * TPG, TG - 1, 1)

        @block.tensor
        def _(pe):
            for pair in range(TT // 2):
                pe.wait_ge(mix_placed, (pair + 1) * (P // C))
                if pair >= 4:
                    pe.wait_ge(h_full_done, pair - 3)
                for i in range(2):
                    pe.wait_ge(x_turned, pair * 2 + i + 1)
                    for kc in range(KC):
                        last = nc.tensor.matmul(
                            bank[:, pair % 4 * 2 + i, kc * P:(kc + 1) * P],
                            x_col[:, pair % RING, i, kc * P:(kc + 1) * P],
                            mix_pair[:, pair * 2 + i, :, :].rearrange("p b d -> p (b d)"),
                            start=True, stop=True)
                last.then_inc(h_ready, 1)
            pe.wait_ge(h_full_done, TT // 2)

            def thrice(ps, terms, h_before=None):
                for n, (a_hi, a_lo, b_hi, b_lo, b_hi_for_lo) in enumerate(terms):
                    if h_before is not None:
                        pe.wait_ge(h_lo_done, h_before + n + 1)
                    nc.tensor.matmul(ps, a_hi, b_hi, start=(n == 0), stop=False)
                    nc.tensor.matmul(ps, a_hi, b_lo, start=False, stop=False)
                    last = nc.tensor.matmul(ps, a_lo, b_hi_for_lo, start=False, stop=(n == len(terms) - 1))
                return last

            def gate_up(par, group, c, h_before=None):
                tokens = bass.ds(group * N, N)
                for n, (ps, ready) in enumerate(((gate_ps[c], gate_ready), (up_ps[c], up_ready))):
                    w = [v[:, :, :].rearrange("p (s n c k g) r -> p s n c k (g r)", s=2, n=3, c=2,
                                              k=KC)[:, par, n, c] for v in (w_hi, w_lo)]
                    thrice(ps, [(w[0][:, kc], w[1][:, kc], h_hi[:, kc, tokens], h_lo[:, kc, tokens],
                                 h_hi[:, kc, tokens]) for kc in range(KC)],
                           h_before if n == 0 else None).then_inc(ready, 1)

            def down(slot, q, half, freed):
                w = [v[:, :, :].rearrange("p (s n b c) r -> p s n c b r", s=2, n=3, c=2)[:, slot, DOWN]
                     for v in (w_hi, w_lo)]
                small = w_down_small[:, :, :].rearrange("p (s b c) r -> p s c b r", s=2, c=2)[:, slot]
                for i in (2 * half, 2 * half + 1):
                    if freed is not None:
                        pe.wait_ge(acc_done, freed + (i + 1))
                    tile = slice(i * P, (i + 1) * P)
                    thrice(bank[:, 4 + i, :],
                           [(inter_hi[:, q, c, tile], inter_lo[:, q, c, tile], w[0][:, c], w[1][:, c], small[:, c])
                            for c in range(2)]).then_inc(down_ready, 1)

            def step(s, par, j, first=False, second=False, last=False):
                for q in range(2):
                    u = number(s, par, j, q)
                    slot = par if q else (j if par else j * -1 + 1)
                    freed = None if first else u * TPG - 2 * TPG
                    follows = not (first and q == 0)
                    pe.wait_ge(w_lo_done, s * (2 * PIECES) + (par * PIECES + 2))
                    if follows:
                        pe.wait_ge(inter_done, u * 2 - 1)
                    gate_up(par, j * 2 + q, 0, (j * 2 + q) * KC if first or second else None)
                    if follows:
                        pe.wait_ge(inter_lo_done, u * 2)
                        if q:
                            pe.wait_ge(w_lo_done, s * (2 * PIECES) + (par + 1) * PIECES)
                            pe.wait_ge(w_small_done, s * 4 + (par + 1) * 2)
                        down(slot, 1 - q, 0, freed)
                        pe.wait_ge(inter_done, u * 2)
                    pe.wait_ge(w_lo_done, s * (2 * PIECES) + (par * PIECES + (4 if first else 5)))
                    gate_up(par, j * 2 + q, 1)
                    if follows:
                        down(slot, 1 - q, 1, freed)

            steps(pe, step)
            pe.wait_ge(inter_lo_done, SC * TG * 2)
            down(1, 1, 0, (SC * TG - 2) * TPG)
            down(1, 1, 1, (SC * TG - 2) * TPG)


_INS = ['x', 'itok_B_1_198', 'L0_cond_weights', 'L0_ffn_gate_W_packed', 'L0_ffn_gate_scales',
        'L0_ffn_up_W_packed', 'L0_ffn_up_scales', 'L0_ffn_down_W_packed', 'L0_ffn_down_scales']


def kernel(**inputs):
    import numpy as np
    import concourse.bacc as bacc
    from concourse.bass_utils import run_bass_kernel_spmd as run

    nc = bacc.Bacc("TRN2", target_bir_lowering=False, num_devices=1)
    arrays, args = {}, []
    for name in _INS:
        a = np.ascontiguousarray(inputs[name])
        arrays[name] = a
        args.append(nc.dram_tensor(name, a.shape, mybir.dt.from_np(a.dtype), kind="ExternalInput").ap())
    out = nc.dram_tensor("out", arrays['x'].shape, F32, kind="ExternalOutput").ap()
    build(nc, *args, out)
    return run(nc, [arrays], core_ids=[0]).results[0]["out"]
```

```python
from contextlib import ExitStack

import concourse.bass as bass
from concourse import mybir

F32 = mybir.dt.float32
F16 = mybir.dt.float16
I32 = mybir.dt.int32
U16 = mybir.dt.uint16
U32 = mybir.dt.uint32
ALU = mybir.AluOpType
ACT = mybir.ActivationFunctionType
AX = mybir.AxisListType

P = 128
G = 4
R = 32
N = 512
LO_UP = 2.0 ** 11
H_EXP = 14
W_EXP = 12
INTER_EXP = -13
LEAST = 2.0 ** -100
EXP_BITS = 0x7F800000
GELU_C = 0.7978845608028654
GELU_A = 0.044715
CODE_MASK = 0x8E00
CODE_EXP = 14


def build(nc, x, itok, cond_w, gate_q, gate_s, up_q, up_s, down_q, down_s, out):
    B, C, H = x.shape
    SAMPLES, _, D = cond_w.shape
    MLP = gate_q.shape[0]
    TOK = B * D
    TG = TOK // N
    TT = TOK // P
    TPG = N // P
    KC = H // P
    SC = MLP // (2 * P)
    BG = 2 * G * KC
    BLK = 3 * BG
    PIECES = 6
    PB = BLK // PIECES
    PW = PB * R
    RING = TT // TPG
    OWN_LO = 2
    SCALES = MLP * H // R // P
    HP = R // 2
    assert C == 64 and D == 64 and BG == 2 * H // R and TG == 4 and SC % 2 == 0

    ctx = ExitStack()
    with ctx:
        def sb(name, shape, dt):
            return ctx.enter_context(nc.sbuf_tensor(name, shape, dt))

        def sem(name):
            return ctx.enter_context(nc.semaphore(name))

        acc = sb("acc", [P, TT, H], F32)
        h_hi = sb("h_hi", [P, KC, TOK], F16)
        h_lo = sb("h_lo", [P, KC, TOK], F16)
        w_hi = sb("w_hi", [P, 2 * BLK, R], F16)
        w_lo = sb("w_lo", [P, 2 * BLK, R], F16)
        w_down_small = sb("w_down_small", [P, 2 * BG, R], F16)
        inter_hi = sb("inter_hi", [P, 2, 2, N], F16)
        inter_lo = sb("inter_lo", [P, 2, 2, N], F16)
        packed = sb("packed", [P, 2 * BLK, HP], I32)
        scales = sb("scales", [P, 2 * BLK], F32)
        shifted = sb("shifted", [P, 2, PB * HP], I32)
        codes = sb("codes", [P, 2, PB * HP], U16)
        w_row = sb("w_row", [P, PW], F32)
        w_col = sb("w_col", [P, 3, PW], F32)
        scale_now = sb("scale_now", [P, PB], F32)
        poly = sb("poly", [P, 2, N], F32)
        tanh = sb("tanh", [P, 2, N], F32)
        inter = sb("inter", [P, 2, N], F32)
        x_col = sb("x_col", [P, RING, 2, H], F32)
        h_full = sb("h_full", [P, KC, TOK], F32)
        all_scales = sb("all_scales", [P, 3, SCALES + 1], F32)
        w_max = sb("w_max", [P, 3], F32)
        w_top = sb("w_top", [P, 3], F32)
        w_factor = sb("w_factor", [P, 3], F32)
        h_max = sb("h_max", [P, TT // 2 + 1], F32)
        h_most = sb("h_most", [P, 1], F32)
        behind = sb("behind", [P, P], I32)
        identity = sb("identity", [P, P], F32)
        ones = sb("ones", [3, P], F32)
        w_largest = sb("w_largest", [3, 1], F32)
        w_diagonal = sb("w_diagonal", [3, 3], F32)
        h_largest = sb("h_largest", [1, 1], F32)
        h_top = sb("h_top", [P, 1], F32)
        h_factor = sb("h_factor", [P, 1], F32)
        gate_unit = sb("gate_unit", [P, 1], F32)
        down_unit = sb("down_unit", [P, 1], F32)
        h_square = sb("h_square", [P, 1], F32)
        w_product = sb("w_product", [P, 1], F32)
        mix = sb("mix", [P, TT, D], F32)
        mix_pair = sb("mix_pair", [P, TT, P // C, D], F32)
        who = sb("who", [P, B], I32)
        held = sb("held", [P, B], I32)
        chan = sb("chan", [P, TT], I32)
        row = sb("row", [P, TT], U32)
        bank = ctx.enter_context(nc.psum_tensor("bank", [P, 8, N], F32))
        rows_ps, all_ps = bank[:, 7, 0:P], bank[:, 7, P:P + 3]
        gate_ps = [bank[:, 0, :], bank[:, 2, :]]
        up_ps = [bank[:, 1, :], bank[:, 3, :]]

        x_loaded = [sem(f"x_loaded{pair}") for pair in range(TT // 2)]
        who_loaded = sem("who_loaded")
        chan_made = sem("chan_made")
        who_held = sem("who_held")
        row_made = sem("row_made")
        scales_loaded = sem("scales_loaded")
        least_set = sem("least_set")
        w_max_done = sem("w_max_done")
        behind_made = sem("behind_made")
        identity_made = sem("identity_made")
        w_max_turned = sem("w_max_turned")
        w_largest_done = sem("w_largest_done")
        w_diagonal_done = sem("w_diagonal_done")
        w_top_done = sem("w_top_done")
        w_power_done = sem("w_power_done")
        w_factor_done = sem("w_factor_done")
        h_full_done = sem("h_full_done")
        h_max_done = sem("h_max_done")
        h_most_done = sem("h_most_done")
        h_most_turned = sem("h_most_turned")
        h_largest_done = sem("h_largest_done")
        h_top_done = sem("h_top_done")
        h_power_done = sem("h_power_done")
        h_factor_done = sem("h_factor_done")
        unit_done = sem("unit_done")
        units_ready = sem("units_ready")
        w_small_done = sem("w_small_done")
        mix_cleared = sem("mix_cleared")
        mix_placed = sem("mix_placed")
        mix_loaded = [sem(f"mix_loaded{pair}") for pair in range(TT // 2)]
        packed_loaded = [[sem(f"packed_loaded{p}{k}") for k in range(3)] for p in range(2)]
        x_turned = sem("x_turned")
        h_ready = sem("h_ready")
        h_hi_done = sem("h_hi_done")
        h_scaled_done = sem("h_scaled_done")
        h_lo_done = sem("h_lo_done")
        shift_done = sem("shift_done")
        codes_done = sem("codes_done")
        scale_done = sem("scale_done")
        w_row_done = sem("w_row_done")
        w_col_done = sem("w_col_done")
        w_hi_done = sem("w_hi_done")
        w_lo_done = sem("w_lo_done")
        gate_ready = sem("gate_ready")
        up_ready = sem("up_ready")
        square_done = sem("square_done")
        poly_done = sem("poly_done")
        arg_done = sem("arg_done")
        tanh_done = sem("tanh_done")
        gelu_done = sem("gelu_done")
        inter_done = sem("inter_done")
        inter_hi_done = sem("inter_hi_done")
        inter_lo_done = sem("inter_lo_done")
        down_ready = sem("down_ready")
        acc_done = sem("acc_done")
        stored = sem("stored")

        x_tok = x.rearrange("(t b) c h -> t (b c) h", b=P // C)
        out_tok = out.rearrange("(t b) c h -> t (b c) h", b=P // C)

        LOADS = 2 * G

        def steps(eng, step):
            step(0, 0, 0, first=True)
            step(0, 0, 1, second=True)
            with eng.Fori(0, 2) as j:
                step(0, 1, j)
            with eng.Fori(1, SC // 2 - 1) as s:
                with eng.Fori(0, 2) as j:
                    step(s, 0, j)
                with eng.Fori(0, 2) as j:
                    step(s, 1, j)
            with eng.Fori(0, 2) as j:
                step(SC // 2 - 1, 0, j)
            with eng.Fori(0, 2) as j:
                step(SC // 2 - 1, 1, j, last=True)

        def number(s, par, j, q):
            return s * (2 * TG) + j * 2 + (par * TG + q)

        GATE, UP, DOWN = range(3)

        def stored_piece(t, slot, kind, half):
            if kind == DOWN:
                return t.rearrange("p (s n h o m) w -> p s n h o (m w)", s=2, n=3, h=2, o=1)[:, slot, kind, half]
            return t.rearrange("p (s n g c k) w -> p s n c g (k w)", s=2, n=3, c=2, k=KC)[:, slot, kind, half]

        def weight_piece(t, slot, kind, half):
            if kind == DOWN:
                return t.rearrange("p (s n h a k) r -> p s n h a k r", s=2, n=3, h=2, k=KC)[:, slot, kind, half]
            return t.rearrange("p (s n c k g) r -> p s n c g k r", s=2, n=3, c=2, k=KC)[:, slot, kind, half]

        def in_blocks(t):
            return t.rearrange("p (a k r) -> p a k r", k=KC, r=R)

        def piece(s, par, j, kind):
            return s * (2 * PIECES) + j * 3 + (par * PIECES + kind), par % 2, kind, j

        FIRST = [(0, 0, GATE, 0), (1, 0, UP, 0), (2, 0, GATE, 1), (3, 0, UP, 1),
                 (4, 0, DOWN, 0), (5, 0, DOWN, 1)]

        block = ctx.enter_context(nc.Block())

        @block.sync
        def _(sp):
            sp.dma_start(who[:, :], itok.rearrange("(o b) -> o b", o=1).to_broadcast([P, B])
                         ).then_inc(who_loaded, 16)

            def load(sc, par, kind):
                words, scale = ((gate_q, gate_s), (up_q, up_s), (down_q, down_s))[kind]
                rows = bass.ds(sc * (2 * P), 2 * P)
                blocks = slice(par * BLK + kind * BG, par * BLK + (kind + 1) * BG)
                run = 2 if kind == DOWN else KC
                for g in range(G):
                    to = slice(g * R, (g + 1) * R)
                    if kind == DOWN:
                        w_from = words[:, bass.ds(sc * (2 * G * HP) + g * 2 * HP, 2 * HP)]
                        s_from = scale[:, bass.ds(sc * (2 * G) + g * 2, 2)]
                    else:
                        w_from = words[rows, g * KC * HP:(g + 1) * KC * HP]
                        s_from = scale[rows, g * KC:(g + 1) * KC]
                    sp.dma_start(packed[to, blocks, :].rearrange("r (b k) w -> r b (k w)", k=run),
                                 w_from.rearrange("(b r) w -> r b w", r=R)).then_inc(packed_loaded[par][kind], 16)
                    sp.dma_start(scales[to, blocks].rearrange("r (b k) -> r b k", k=run),
                                 s_from.rearrange("(b r) k -> r b k", r=R)).then_inc(packed_loaded[par][kind], 16)

            def load_x(pair):
                tiles = slice(pair * 2, pair * 2 + 2)
                sp.dma_start(acc[:, tiles, :], x_tok[tiles].rearrange("t p h -> p t h")
                             ).then_inc(x_loaded[pair], 16)

            load_x(0)
            load_x(1)
            load_x(2)
            load(0, 0, GATE)
            load_x(3)
            load(0, 0, UP)
            for pair in range(4, TT // 2):
                sp.wait_ge(x_turned, (pair - 2) * 2)
                load_x(pair)
            load(0, 0, DOWN)
            for kind in (GATE, UP, DOWN):
                load(1, 1, kind)
            with sp.Fori(1, SC // 2) as s:
                for par in range(2):
                    sp.wait_ge(w_row_done, s * (2 * PIECES) - (1 - par) * PIECES)
                    for kind in (GATE, UP, DOWN):
                        load(s * 2 + par, par, kind)
            for t in range(TT):
                sp.wait_ge(acc_done, (SC - 1) * TT + t + 1)
                sp.dma_start(out_tok[t], acc[:, t, :]).then_inc(stored, 16)
            sp.wait_ge(stored, 16 * TT)

        @block.gpsimd
        def _(pool):
            for b in range(P // C):
                nc.gpsimd.iota(chan[b * C:(b + 1) * C, :], [[0, TT]], base=0,
                               channel_multiplier=1).then_inc(chan_made, 1)
            pool.wait_ge(chan_made, P // C)
            nc.gpsimd.iota(behind[:, :], [[1, P]], base=0, channel_multiplier=-1).then_inc(behind_made, 1)

            def gather(t):
                pool.indirect_dma_start(
                    out=mix[:, t, :], out_offset=None,
                    in_=cond_w.rearrange("s c d -> (s c) d"),
                    in_offset=bass.IndirectOffsetOnAxis(ap=row[:, t:t + 1], axis=0)
                ).then_inc(mix_loaded[t // 2], 16)

            def weights_lo(n, slot, kind, half):
                pool.wait_ge(w_hi_done, n + 1)
                nc.gpsimd.tensor_tensor(weight_piece(w_lo, slot, kind, half), in_blocks(w_col[:, kind, :]),
                                        weight_piece(w_hi, slot, kind, half),
                                        ALU.subtract).then_inc(w_lo_done, 1)

            def hidden_lo(t, kc):
                pool.wait_ge(h_scaled_done, t * KC + kc + 1 - OWN_LO)
                part = (slice(None), kc, slice(t * N, (t + 1) * N))
                nc.gpsimd.tensor_tensor(h_lo[part], h_full[part], h_hi[part],
                                        ALU.subtract).then_inc(h_lo_done, 1)

            pool.wait_ge(row_made, P // C)
            for t in range(TT):
                gather(t)
            weights_lo(*FIRST[0])
            weights_lo(*FIRST[1])
            pool.wait_ge(h_lo_done, OWN_LO)
            for kc in range(OWN_LO, KC):
                hidden_lo(0, kc)
            weights_lo(*FIRST[2])
            weights_lo(*FIRST[3])
            hidden_lo(1, 0)
            weights_lo(*FIRST[4])
            for kc in (1, 2, 3):
                hidden_lo(1, kc)
            weights_lo(*FIRST[5])
            for kc in range(KC):
                hidden_lo(2, kc)
            for kc in (0, 1, 2):
                hidden_lo(3, kc)

            def step(s, par, j, first=False, second=False, last=False):
                if not last:
                    for kind in (GATE, UP, DOWN):
                        weights_lo(*piece(s, par + 1, j, kind))
                    if first:
                        hidden_lo(3, 3)

            steps(pool, step)

        @block.scalar
        def _(act):
            for kind, scale in enumerate((gate_s, up_s, down_s)):
                act.dma_start(all_scales[:, kind, 0:SCALES],
                              scale.rearrange("(p n) k -> p (n k)", p=P)).then_inc(scales_loaded, 16)

            def turn_x(pair):
                act.wait_ge(x_loaded[pair], 16)
                if pair >= RING:
                    act.wait_ge(h_ready, pair - RING + 1)
                for i in range(2):
                    nc.scalar.activation(
                        x_col[:, pair % RING, i, :].rearrange("p (k g r) -> p g k r", k=KC, r=R),
                        acc[:, pair * 2 + i, :].rearrange("p (g k r) -> p g k r", k=KC, r=R),
                        ACT.Copy).then_inc(x_turned, 1)

            def keep_h(pair):
                act.wait_ge(h_ready, pair + 1)
                nc.scalar.activation(
                    h_full[:, :, pair * 2 * P:(pair + 1) * 2 * P].rearrange("p k (i t) -> p i k t", i=2),
                    bank[:, pair % 4 * 2:pair % 4 * 2 + 2, :].rearrange("p i (k t) -> p i k t", k=KC),
                    ACT.Copy).then_inc(h_full_done, 1)

            def weights_hi(n, slot, kind, half):
                act.wait_ge(w_col_done, n + 1)
                hi = weight_piece(w_hi, slot, kind, half)
                nc.scalar.activation(hi, in_blocks(w_col[:, kind, :]), ACT.Copy).then_inc(w_hi_done, 1)
                if kind == DOWN:
                    act.wait_ge(w_hi_done, n + 1)
                    nc.scalar.activation(
                        w_down_small[:, :, :].rearrange("p (s h a k) r -> p s h a k r", s=2, h=2, k=KC)[:, slot, half],
                        hi, ACT.Copy, scale=1.0 / LO_UP).then_inc(w_small_done, 1)

            def hidden_hi(t, kc):
                part = (slice(None), kc, slice(t * N, (t + 1) * N))
                nc.scalar.activation(h_hi[part], h_full[part], ACT.Copy,
                                     scale=h_factor[:, :]).then_inc(h_hi_done, 1)
                if t * KC + kc >= OWN_LO:
                    act.wait_ge(h_hi_done, t * KC + kc + 1)
                    nc.scalar.activation(h_full[part], h_full[part], ACT.Copy,
                                         scale=h_factor[:, :]).then_inc(h_scaled_done, 1)

            for pair in range(RING):
                turn_x(pair)
            for pair in range(3):
                keep_h(pair)
                turn_x(pair + RING)
            weights_hi(*FIRST[0])
            keep_h(3)
            keep_h(4)
            turn_x(7)
            for pair in range(5, TT // 2):
                keep_h(pair)
            weights_hi(*FIRST[1])
            act.wait_ge(h_factor_done, 1)
            act.wait_ge(h_full_done, TT // 2)
            for kc in range(KC):
                hidden_hi(0, kc)
            weights_hi(*FIRST[2])
            weights_hi(*FIRST[3])
            hidden_hi(1, 0)
            left = {(0, 0): ([(1, 1)], [(1, 2), (1, 3)]), (0, 1): ([(2, 0)], [(2, 1)]),
                    (1, 0): ([(2, 2)], [(2, 3)]), (1, 1): ([(3, 0)], [(3, 1), (3, 2)]),
                    (2, 0): ([(3, 3)], [])}
            act.wait_ge(units_ready, 1)

            def step(s, par, j, first=False, second=False, last=False):
                for q in range(2):
                    u = number(s, par, j, q)
                    for c in range(2):
                        act.wait_ge(gate_ready, u * 2 + (c + 1))
                        nc.scalar.activation(poly[:, c, :], gate_ps[c], ACT.Square,
                                             scale=gate_unit[:, :]).then_inc(square_done, 1)
                        if first and q == 0:
                            weights_hi(*FIRST[4 + c])
                        elif first:
                            weights_hi(*piece(s, par + 1, j, UP if c else GATE))
                        elif c == 1 and not last:
                            weights_hi(*piece(s, par + 1, j, DOWN if q else GATE))
                        act.wait_ge(arg_done, u * 2 + (c + 1))
                        nc.scalar.activation(tanh[:, c, :], tanh[:, c, :], ACT.Tanh).then_inc(tanh_done, 1)
                        before_inter, behind_inter = left.get((u, c), ([], [])) if first or second else ([], [])
                        for chunk in before_inter:
                            hidden_hi(*chunk)
                        act.wait_ge(inter_done, u * 2 + (c + 1))
                        if not first:
                            act.wait_ge(down_ready, u * TPG - TPG)
                        nc.scalar.activation(inter_hi[:, q, c, :], inter[:, c, :], ACT.Copy,
                                             scale=1.0 / LO_UP).then_inc(inter_hi_done, 1)
                        for chunk in behind_inter:
                            hidden_hi(*chunk)
                    if first and q:
                        weights_hi(*piece(s, par + 1, j, DOWN))
                    elif not (first or last) and q == 0:
                        weights_hi(*piece(s, par + 1, j, UP))

            steps(act, step)

        @block.vector
        def _(dve):
            nc.vector.memset(mix_pair[:, :, :, :], 0.0).then_inc(mix_cleared, 1)
            dve.wait_ge(who_loaded, 16)
            nc.vector.tensor_scalar(held[:, :], who[:, :], 0.0, float(SAMPLES - 1), ALU.max,
                                    ALU.min).then_inc(who_held, 1)
            dve.wait_ge(who_held, 1)
            dve.wait_ge(chan_made, P // C)
            for b in range(P // C):
                half = slice(b * C, (b + 1) * C)
                nc.vector.scalar_tensor_tensor(row[half, :], held[half, :].rearrange("p (t b) -> p b t", b=P // C)[:, b],
                                               float(C), chan[half, :], ALU.mult, ALU.add).then_inc(row_made, 1)

            nc.vector.memset(all_scales[:, :, SCALES:], LEAST).then_inc(least_set, 1)
            nc.vector.memset(h_max[:, TT // 2:], LEAST).then_inc(least_set, 1)
            nc.vector.memset(ones[:, :], 1.0).then_inc(identity_made, 1)
            dve.wait_ge(behind_made, 1)
            nc.vector.tensor_scalar(identity[:, :], behind[:, :], 0.0, None, ALU.is_equal).then_inc(identity_made, 1)

            def unpack(n, slot, kind, half, loads):
                dve.wait_ge(packed_loaded[slot][kind], loads * (16 * LOADS))
                runs = 1 if kind == DOWN else G
                for t in range(2):
                    nc.vector.tensor_scalar(shifted[:, t, :].rearrange("p (a w) -> p a w", a=runs),
                                            stored_piece(packed, slot, kind, half), 28 - 4 * t, 3,
                                            ALU.logical_shift_left,
                                            ALU.arith_shift_right).then_inc(shift_done, 1)

            def mask(n, slot, kind, half):
                dve.wait_ge(shift_done, n * 2 + 2)
                nc.vector.tensor_scalar(codes[:, :, :],
                                        shifted[:, :, :].bitcast(U16).rearrange("p t (w e) -> p t w e", e=2)[:, :, :, 1],
                                        CODE_MASK, None, ALU.bitwise_and).then_inc(codes_done, 1)
                runs = 1 if kind == DOWN else G
                nc.vector.tensor_scalar(scale_now[:, :].rearrange("p (a k) -> p a k", a=runs),
                                        stored_piece(scales[:, :].unsqueeze(2), slot, kind, half),
                                        w_factor[:, kind:kind + 1], None, ALU.mult).then_inc(scale_done, 1)

            def scale(n, slot, kind, half):
                dve.wait_ge(codes_done, n + 1)
                dve.wait_ge(scale_done, n + 1)
                nc.vector.tensor_tensor(
                    w_row[:, :].rearrange("p (b i t) -> p t b i", t=2, i=HP),
                    codes[:, :, :].bitcast(F16).rearrange("p t (b i) -> p t b i", i=HP),
                    scale_now[:, :].unsqueeze(1).unsqueeze(3).to_broadcast([P, 2, PB, HP]),
                    ALU.mult).then_inc(w_row_done, 1)

            def turn(n, slot, kind, half, before=3):
                dve.wait_ge(w_row_done, n + 1)
                if before:
                    dve.wait_ge(w_lo_done, n - (before - 1))
                nc.vector.transpose(w_col[:, kind, :], w_row[:, :]).then_inc(w_col_done, 1)

            def whole_piece(p, before=0):
                unpack(*p, 1)
                mask(*p)
                scale(*p)
                turn(*p, before)

            def largest_h(pair):
                dve.wait_ge(h_full_done, pair + 1)
                nc.vector.tensor_reduce(h_max[:, pair:pair + 1], h_full[:, :, pair * 2 * P:(pair + 1) * 2 * P],
                                        AX.XY, ALU.max, apply_absolute_value=True).then_inc(h_max_done, 1)

            def power(top, n, done):
                nc.vector.tensor_scalar(top[:, :].bitcast(I32), all_ps[:, 0:n].bitcast(I32), EXP_BITS, None,
                                        ALU.bitwise_and).then_inc(done, 1)
                dve.wait_ge(done, 1)

            def inverse(out, top, exp, done):
                nc.vector.tensor_scalar(out[:, :].bitcast(I32), top[:, :].bitcast(I32), -1.0,
                                        float((254 + exp) << 23), ALU.mult, ALU.add).then_inc(done, 1)

            def hidden_lo():
                for kc in range(OWN_LO):
                    part = (slice(None), kc, slice(0, N))
                    dve.wait_ge(h_hi_done, kc + 1)
                    nc.vector.scalar_tensor_tensor(h_lo[part], h_full[part], h_factor[:, :], h_hi[part],
                                                   ALU.mult, ALU.subtract).then_inc(h_lo_done, 1)

            def place_mix(pair):
                dve.wait_ge(mix_loaded[pair], 16 * 2)
                for b in range(P // C):
                    part = (slice(b * C, (b + 1) * C), slice(pair * 2, pair * 2 + 2))
                    nc.vector.tensor_copy(mix_pair[part + (b,)], mix[part]).then_inc(mix_placed, 1)

            dve.wait_ge(scales_loaded, 16 * 3)
            dve.wait_ge(least_set, 2)
            nc.vector.tensor_reduce(w_max[:, :], all_scales[:, :, :], AX.X, ALU.max,
                                    apply_absolute_value=True).then_inc(w_max_done, 1)
            dve.wait_ge(w_max_turned, 1)
            nc.vector.tensor_reduce(w_largest[:, :], rows_ps[0:3], AX.X, ALU.max).then_inc(w_largest_done, 1)
            dve.wait_ge(w_largest_done, 1)
            nc.vector.tensor_scalar(w_diagonal[:, :], identity[0:3, 0:3], w_largest[:, :], None,
                                    ALU.mult).then_inc(w_diagonal_done, 1)
            dve.wait_ge(mix_cleared, 1)
            place_mix(0)
            dve.wait_ge(w_top_done, 1)
            power(w_top, 3, w_power_done)
            inverse(w_factor, w_top, W_EXP + CODE_EXP, w_factor_done)
            dve.wait_ge(w_factor_done, 1)
            unpack(*FIRST[0], 1)
            mask(*FIRST[0])
            scale(*FIRST[0])
            place_mix(1)
            turn(*FIRST[0], 0)
            place_mix(2)
            whole_piece(FIRST[1])
            for pair in range(3, TT // 2):
                place_mix(pair)
                if pair == 6:
                    unpack(*FIRST[2], 1)
                    mask(*FIRST[2])
                largest_h(pair - 3)
            for pair in range(TT // 2 - 3, TT // 2):
                largest_h(pair)
            dve.wait_ge(h_max_done, TT // 2)
            nc.vector.tensor_reduce(h_most[:, :], h_max[:, :], AX.X, ALU.max).then_inc(h_most_done, 1)
            nc.vector.tensor_scalar(w_product[:, :], w_top[:, 0:1], w_top[:, 1:2], w_top[:, 2:3],
                                    ALU.mult, ALU.mult).then_inc(unit_done, 1)
            scale(*FIRST[2])
            dve.wait_ge(h_most_turned, 1)
            nc.vector.tensor_reduce(h_largest[:, :], rows_ps[0:1], AX.X, ALU.max).then_inc(h_largest_done, 1)
            turn(*FIRST[2], 2)
            dve.wait_ge(h_top_done, 1)
            power(h_top, 1, h_power_done)
            inverse(h_factor, h_top, H_EXP, h_factor_done)
            nc.vector.tensor_scalar(gate_unit[:, :], h_top[:, :], w_top[:, 0:1], 2.0 ** -(H_EXP + W_EXP),
                                    ALU.mult, ALU.mult).then_inc(unit_done, 1)
            nc.vector.tensor_scalar(h_square[:, :], h_top[:, :], h_top[:, :], 2.0 ** -(INTER_EXP + W_EXP),
                                    ALU.mult, ALU.mult).then_inc(unit_done, 1)
            dve.wait_ge(unit_done, 3)
            nc.vector.tensor_tensor(down_unit[:, :], h_square[:, :], w_product[:, :], ALU.mult).then_inc(units_ready, 1)
            unpack(*FIRST[3], 1)
            dve.wait_ge(h_factor_done, 1)
            dve.wait_ge(units_ready, 1)
            hidden_lo()
            mask(*FIRST[3])
            scale(*FIRST[3])
            turn(*FIRST[3], 2)
            whole_piece(FIRST[4])

            def gelu(n, c):
                dve.wait_ge(square_done, n)
                nc.vector.tensor_scalar(poly[:, c, :], poly[:, c, :], GELU_C * GELU_A, GELU_C,
                                        ALU.mult, ALU.add).then_inc(poly_done, 1)
                dve.wait_ge(poly_done, n)
                nc.vector.scalar_tensor_tensor(tanh[:, c, :], gate_ps[c], gate_unit[:, :], poly[:, c, :],
                                               ALU.mult, ALU.mult).then_inc(arg_done, 1)
                dve.wait_ge(tanh_done, n)
                nc.vector.scalar_tensor_tensor(tanh[:, c, :], tanh[:, c, :], 1.0, gate_ps[c],
                                               ALU.add, ALU.mult).then_inc(gelu_done, 1)
                dve.wait_ge(gelu_done, n)
                dve.wait_ge(up_ready, n)
                nc.vector.scalar_tensor_tensor(
                    inter[:, c, :], tanh[:, c, :], 0.5 * LO_UP * 2.0 ** (INTER_EXP - 2 * (H_EXP + W_EXP)),
                    up_ps[c], ALU.mult, ALU.mult).then_inc(inter_done, 1)

            def split_lo(n, q, c):
                dve.wait_ge(inter_hi_done, n)
                nc.vector.scalar_tensor_tensor(inter_lo[:, q, c, :], inter_hi[:, q, c, :], -LO_UP, inter[:, c, :],
                                               ALU.mult, ALU.add).then_inc(inter_lo_done, 1)

            def add_down(done, group, half):
                for i in (2 * half, 2 * half + 1):
                    dve.wait_ge(down_ready, done + (i + 1))
                    tile = acc[:, bass.ds(group * TPG + i, 1), :].rearrange("p o h -> p (o h)")
                    nc.vector.scalar_tensor_tensor(tile, bank[:, 4 + i, :], down_unit[:, :], tile,
                                                   ALU.mult, ALU.add).then_inc(acc_done, 1)

            def step(s, par, j, first=False, second=False, last=False):
                for q in range(2):
                    u = number(s, par, j, q)
                    group = j * 2 if q else j * -2 + 3
                    p, p_up = piece(s, par + 1, j, DOWN if q else GATE), piece(s, par + 1, j, UP)
                    loads = s + ((par + 1) // 2 + 1)
                    if first:
                        gelu(u * 2 + 1, 0)
                        split_lo(u * 2 + 1, q, 0)
                        if q:
                            add_down(u * TPG - TPG, group, 0)
                            whole_piece(piece(s, par + 1, j, UP), 3)
                        else:
                            whole_piece(FIRST[5], 1)
                        gelu(u * 2 + 2, 1)
                        split_lo(u * 2 + 2, q, 1)
                        if q:
                            whole_piece(piece(s, par + 1, j, DOWN), 3)
                            add_down(u * TPG - TPG, group, 1)
                        else:
                            whole_piece(piece(s, par + 1, j, GATE), 3)
                        continue
                    if not last:
                        unpack(*p, loads)
                    gelu(u * 2 + 1, 0)
                    if not last:
                        mask(*p)
                    split_lo(u * 2 + 1, q, 0)
                    add_down(u * TPG - TPG, group, 0)
                    if not last:
                        scale(*p)
                        turn(*p)
                        if q == 0:
                            unpack(*p_up, loads)
                    gelu(u * 2 + 2, 1)
                    if not last and q == 0:
                        mask(*p_up)
                    split_lo(u * 2 + 2, q, 1)
                    if not last and q == 0:
                        scale(*p_up)
                        turn(*p_up)
                    add_down(u * TPG - TPG, group, 1)

            steps(dve, step)
            add_down((SC * TG - 1) * TPG, TG - 1, 0)
            add_down((SC * TG - 1) * TPG, TG - 1, 1)

        @block.tensor
        def _(pe):
            def for_all(maxima, n, made, turned, top, top_made, done):
                pe.wait_ge(made, 1)
                nc.tensor.matmul(rows_ps[0:n], maxima[:, :], identity[:, :], start=True, stop=True).then_inc(turned, 1)
                pe.wait_ge(top_made, 1)
                nc.tensor.matmul(all_ps[:, 0:n], ones[0:n, :], top[:, :], start=True, stop=True).then_inc(done, 1)

            pe.wait_ge(identity_made, 2)
            for_all(w_max, 3, w_max_done, w_max_turned, w_diagonal, w_diagonal_done, w_top_done)
            for pair in range(TT // 2):
                pe.wait_ge(mix_placed, (pair + 1) * (P // C))
                if pair == 3:
                    pe.wait_ge(w_power_done, 1)
                if pair >= 4:
                    pe.wait_ge(h_full_done, pair - 3)
                for i in range(2):
                    pe.wait_ge(x_turned, pair * 2 + i + 1)
                    for kc in range(KC):
                        last = nc.tensor.matmul(
                            bank[:, pair % 4 * 2 + i, kc * P:(kc + 1) * P],
                            x_col[:, pair % RING, i, kc * P:(kc + 1) * P],
                            mix_pair[:, pair * 2 + i, :, :].rearrange("p b d -> p (b d)"),
                            start=True, stop=True)
                last.then_inc(h_ready, 1)
            pe.wait_ge(h_full_done, TT // 2)
            for_all(h_most, 1, h_most_done, h_most_turned, h_largest, h_largest_done, h_top_done)

            def thrice(ps, terms, h_before=None):
                for n, (a_hi, a_lo, b_hi, b_lo, b_hi_for_lo) in enumerate(terms):
                    if h_before is not None:
                        pe.wait_ge(h_lo_done, h_before + n + 1)
                    nc.tensor.matmul(ps, a_hi, b_hi, start=(n == 0), stop=False)
                    nc.tensor.matmul(ps, a_hi, b_lo, start=False, stop=False)
                    last = nc.tensor.matmul(ps, a_lo, b_hi_for_lo, start=False, stop=(n == len(terms) - 1))
                return last

            def gate_up(par, group, c, h_before=None):
                tokens = bass.ds(group * N, N)
                for n, (ps, ready) in enumerate(((gate_ps[c], gate_ready), (up_ps[c], up_ready))):
                    w = [v[:, :, :].rearrange("p (s n c k g) r -> p s n c k (g r)", s=2, n=3, c=2,
                                              k=KC)[:, par, n, c] for v in (w_hi, w_lo)]
                    thrice(ps, [(w[0][:, kc], w[1][:, kc], h_hi[:, kc, tokens], h_lo[:, kc, tokens],
                                 h_hi[:, kc, tokens]) for kc in range(KC)],
                           h_before if n == 0 else None).then_inc(ready, 1)

            def down(slot, q, half, freed):
                w = [v[:, :, :].rearrange("p (s n b c) r -> p s n c b r", s=2, n=3, c=2)[:, slot, DOWN]
                     for v in (w_hi, w_lo)]
                small = w_down_small[:, :, :].rearrange("p (s b c) r -> p s c b r", s=2, c=2)[:, slot]
                for i in (2 * half, 2 * half + 1):
                    if freed is not None:
                        pe.wait_ge(acc_done, freed + (i + 1))
                    tile = slice(i * P, (i + 1) * P)
                    thrice(bank[:, 4 + i, :],
                           [(inter_hi[:, q, c, tile], inter_lo[:, q, c, tile], w[0][:, c], w[1][:, c], small[:, c])
                            for c in range(2)]).then_inc(down_ready, 1)

            def step(s, par, j, first=False, second=False, last=False):
                for q in range(2):
                    u = number(s, par, j, q)
                    slot = par if q else (j if par else j * -1 + 1)
                    freed = None if first else u * TPG - 2 * TPG
                    follows = not (first and q == 0)
                    pe.wait_ge(w_lo_done, s * (2 * PIECES) + (par * PIECES + 2))
                    if follows:
                        pe.wait_ge(inter_done, u * 2 - 1)
                    gate_up(par, j * 2 + q, 0, (j * 2 + q) * KC if first or second else None)
                    if follows:
                        pe.wait_ge(inter_lo_done, u * 2)
                        if q:
                            pe.wait_ge(w_lo_done, s * (2 * PIECES) + (par + 1) * PIECES)
                            pe.wait_ge(w_small_done, s * 4 + (par + 1) * 2)
                        down(slot, 1 - q, 0, freed)
                        pe.wait_ge(inter_done, u * 2)
                    pe.wait_ge(w_lo_done, s * (2 * PIECES) + (par * PIECES + (4 if first else 5)))
                    gate_up(par, j * 2 + q, 1)
                    if follows:
                        down(slot, 1 - q, 1, freed)

            steps(pe, step)
            pe.wait_ge(inter_lo_done, SC * TG * 2)
            down(1, 1, 0, (SC * TG - 2) * TPG)
            down(1, 1, 1, (SC * TG - 2) * TPG)


_INS = ['x', 'itok_B_1_198', 'L0_cond_weights', 'L0_ffn_gate_W_packed', 'L0_ffn_gate_scales',
        'L0_ffn_up_W_packed', 'L0_ffn_up_scales', 'L0_ffn_down_W_packed', 'L0_ffn_down_scales']


def kernel(**inputs):
    import numpy as np
    import concourse.bacc as bacc
    from concourse.bass_utils import run_bass_kernel_spmd as run

    nc = bacc.Bacc("TRN2", target_bir_lowering=False, num_devices=1)
    arrays, args = {}, []
    for name in _INS:
        a = np.ascontiguousarray(inputs[name])
        arrays[name] = a
        args.append(nc.dram_tensor(name, a.shape, mybir.dt.from_np(a.dtype), kind="ExternalInput").ap())
    out = nc.dram_tensor("out", arrays['x'].shape, F32, kind="ExternalOutput").ap()
    build(nc, *args, out)
    return run(nc, [arrays], core_ids=[0]).results[0]["out"]
```
